# Optimizing a Trainium2 kernel written in Bass

```python
import numpy as np
import jax
import jax.numpy as jnp

def _softmax(x, axis=-1):
    return jax.nn.softmax(x, axis=axis)

def _gelu(x):
    return jax.nn.gelu(x, approximate=True)

def _silu(x):
    return jax.nn.silu(x)

def _sigmoid(x):
    return jax.nn.sigmoid(x)

def _layernorm(x, axis=-1, eps=1e-05):
    m = jnp.mean(x, axis=axis, keepdims=True)
    v = jnp.var(x, axis=axis, keepdims=True)
    return (x - m) / jnp.sqrt(v + eps)

def _scatter_add(tgt, idx, src, axis=0):
    return tgt.at[idx].add(src)

def _segment_sum(src, seg, n):
    return jax.ops.segment_sum(src, seg, n)
kernel_name = 'mk_adj_ffn_d2_adj_r2_12278a'

def setup_inputs(seed: int=0):
    np.random.seed(seed)
    _w = jnp.asarray

    def _rec_inputs():
        import jax
        import jax.numpy as jnp
        _gk = jax.random.key(seed)
        x = -2.104e-05 + 0.9999 * jax.random.normal(jax.random.fold_in(_gk, 1), (16, 512, 128), jnp.float32)
        _a = jax.random.bernoulli(jax.random.fold_in(_gk, 2), 0.0078125, (512, 512))
        _a = jnp.logical_or(_a, jnp.swapaxes(_a, -1, -2))
        _af = _a.astype(jnp.float32)
        _af = _af / jnp.maximum(_af.sum(-1, keepdims=True), 1.0)
        adj = _af
        return (x, adj)
    x, adj = _rec_inputs()

    def _L0_gnn_setup():
        import jax, jax.numpy as jnp
        import numpy as np
        N = 3445
        B = 32
        IN_DIM = 128
        HID_DIM = 128

        def _make_adj(key):
            a = jax.random.uniform(key, (N, N), dtype=jnp.float32)
            a = (a < 0.001).astype(jnp.float32)
            a = jnp.maximum(a, a.T)
            deg = jnp.sum(a, axis=1, keepdims=True)
            return a / jnp.maximum(deg, 1.0)

        def _graph_conv(x, adj, w_loop, w_neigh, b):
            loop = jnp.einsum('bnd,dh->bnh', x, w_loop)
            neigh = jnp.einsum('nm,bmh->bnh', adj, jnp.einsum('bnd,dh->bnh', x, w_neigh))
            return loop + neigh + b
        key = jax.random.key(seed)
        k = jax.random.split(key, 8)
        s1 = 1.0 / np.sqrt(IN_DIM)
        s2 = 1.0 / np.sqrt(HID_DIM)
        return {'x': jax.random.normal(k[0], (B, N, IN_DIM), dtype=jnp.float32), 'adj': _make_adj(k[1]), 'w1_loop': jax.random.normal(k[2], (IN_DIM, HID_DIM), dtype=jnp.float32) * s1, 'w1_neigh': jax.random.normal(k[3], (IN_DIM, HID_DIM), dtype=jnp.float32) * s1, 'b1': jnp.zeros((HID_DIM,), dtype=jnp.float32), 'w2_loop': jax.random.normal(k[4], (HID_DIM, IN_DIM), dtype=jnp.float32) * s2, 'w2_neigh': jax.random.normal(k[5], (HID_DIM, IN_DIM), dtype=jnp.float32) * s2, 'b2': jnp.zeros((IN_DIM,), dtype=jnp.float32)}
    _L0_gnn_all = _L0_gnn_setup()
    _L0_gnn_in = {k: v for k, v in _L0_gnn_all.items() if k in ('w1_loop', 'w1_neigh', 'b1', 'w2_loop', 'w2_neigh', 'b2')}
    del _L0_gnn_all

    def _L0_ffn_setup():
        import jax, jax.numpy as jnp
        import numpy as np
        E, D, H, TOP_K = (6, 128, 128, 2)
        ROUTER_H = D // 2
        key = jax.random.key(seed)
        ks = jax.random.split(key, 12)
        s = 1.0 / np.sqrt(D)
        sh = 1.0 / np.sqrt(H)
        sr = 1.0 / np.sqrt(ROUTER_H)
        return {'features': jax.random.normal(ks[0], (8, 2048, D), dtype=jnp.float32), 'router_w1': jax.random.uniform(ks[1], (D, ROUTER_H), jnp.float32, -s, s), 'router_b1': jnp.zeros((ROUTER_H,), jnp.float32), 'router_w2': jax.random.uniform(ks[2], (ROUTER_H, E), jnp.float32, -sr, sr), 'router_b2': jnp.zeros((E,), jnp.float32), 'expert_w1': jax.random.uniform(ks[3], (E, D, H), jnp.float32, -s, s), 'expert_b1': jnp.zeros((E, H), jnp.float32), 'expert_w2': jax.random.uniform(ks[4], (E, H, H), jnp.float32, -sh, sh), 'expert_b2': jnp.zeros((E, H), jnp.float32), 'expert_w3': jax.random.uniform(ks[5], (E, H, D), jnp.float32, -sh, sh), 'expert_b3': jnp.zeros((E, D), jnp.float32)}
    _L0_ffn_all = _L0_ffn_setup()
    _L0_ffn_in = {k: v for k, v in _L0_ffn_all.items() if k in ('router_w1', 'router_b1', 'router_w2', 'router_b2', 'expert_w1', 'expert_b1', 'expert_w2', 'expert_b2', 'expert_w3', 'expert_b3')}
    del _L0_ffn_all

    def _L1_gnn_setup():
        import jax, jax.numpy as jnp
        import numpy as np
        B, N, H, OUT, RANK = (64, 512, 128, 128, 10)
        ORDER = 2

        def _conv(x, adj):
            return x * jnp.sum(adj, axis=1)[None, :, None]
        key = jax.random.key(seed)
        ks = jax.random.split(key, 6)
        x = jax.random.normal(ks[0], (B, N, H), dtype=jnp.float32)
        support0 = jax.random.uniform(ks[1], (N, N), dtype=jnp.float32)
        support1 = jax.random.uniform(ks[2], (N, N), dtype=jnp.float32)
        node_vec1 = jax.random.normal(ks[3], (N, RANK), dtype=jnp.float32)
        node_vec2 = jax.random.normal(ks[4], (RANK, N), dtype=jnp.float32)
        d_in = (ORDER * 3 + 1) * H
        W = jax.random.normal(ks[5], (d_in, OUT), dtype=jnp.float32) * (1.0 / np.sqrt(d_in))
        b = jnp.zeros((OUT,), dtype=jnp.float32)
        return {'x': x, 'support0': support0, 'support1': support1, 'node_vec1': node_vec1, 'node_vec2': node_vec2, 'W': W, 'b': b}
    _L1_gnn_all = _L1_gnn_setup()
    _L1_gnn_in = {k: v for k, v in _L1_gnn_all.items() if k in ('node_vec1', 'node_vec2', 'W', 'b')}
    del _L1_gnn_all

    def _L1_ffn_setup():
        import jax, jax.numpy as jnp
        import numpy as np
        TOP_K = 2
        LN_EPS = 1e-05
        key = jax.random.key(seed)
        ks = jax.random.split(key, 8)
        B, S, D, E, H = (16, 512, 128, 8, 512)
        x = jax.random.normal(ks[0], (B, S, D), dtype=jnp.float32)
        Wr = jax.random.normal(ks[1], (D, E), dtype=jnp.float32) * 0.1
        br = jnp.zeros((E,), dtype=jnp.float32)
        ln_g = jnp.ones((E, D), dtype=jnp.float32)
        ln_b = jnp.zeros((E, D), dtype=jnp.float32)
        W1 = jax.random.normal(ks[2], (E, D, H), dtype=jnp.float32) * (1.0 / np.sqrt(D))
        b1 = jnp.zeros((E, H), dtype=jnp.float32)
        W2 = jax.random.normal(ks[3], (E, H, D), dtype=jnp.float32) * (1.0 / np.sqrt(H))
        b2 = jnp.zeros((E, D), dtype=jnp.float32)
        return {'x': x, 'Wr': Wr, 'br': br, 'ln_g': ln_g, 'ln_b': ln_b, 'W1': W1, 'b1': b1, 'W2': W2, 'b2': b2}
    _L1_ffn_all = _L1_ffn_setup()
    _L1_ffn_in = {k: v for k, v in _L1_ffn_all.items() if k in ('Wr', 'br', 'ln_g', 'ln_b', 'W1', 'b1', 'W2', 'b2')}
    del _L1_ffn_all
    return {'x': x, 'adj': adj, 'L0_gnn_w1_loop': _L0_gnn_in['w1_loop'], 'L0_gnn_w1_neigh': _L0_gnn_in['w1_neigh'], 'L0_gnn_b1': _L0_gnn_in['b1'], 'L0_gnn_w2_loop': _L0_gnn_in['w2_loop'], 'L0_gnn_w2_neigh': _L0_gnn_in['w2_neigh'], 'L0_gnn_b2': _L0_gnn_in['b2'], 'L0_ffn_router_w1': _L0_ffn_in['router_w1'], 'L0_ffn_router_b1': _L0_ffn_in['router_b1'], 'L0_ffn_router_w2': _L0_ffn_in['router_w2'], 'L0_ffn_router_b2': _L0_ffn_in['router_b2'], 'L0_ffn_expert_w1': _L0_ffn_in['expert_w1'], 'L0_ffn_expert_b1': _L0_ffn_in['expert_b1'], 'L0_ffn_expert_w2': _L0_ffn_in['expert_w2'], 'L0_ffn_expert_b2': _L0_ffn_in['expert_b2'], 'L0_ffn_expert_w3': _L0_ffn_in['expert_w3'], 'L0_ffn_expert_b3': _L0_ffn_in['expert_b3'], 'L1_gnn_node_vec1': _L1_gnn_in['node_vec1'], 'L1_gnn_node_vec2': _L1_gnn_in['node_vec2'], 'L1_gnn_W': _L1_gnn_in['W'], 'L1_gnn_b': _L1_gnn_in['b'], 'L1_ffn_Wr': _L1_ffn_in['Wr'], 'L1_ffn_br': _L1_ffn_in['br'], 'L1_ffn_ln_g': _L1_ffn_in['ln_g'], 'L1_ffn_ln_b': _L1_ffn_in['ln_b'], 'L1_ffn_W1': _L1_ffn_in['W1'], 'L1_ffn_b1': _L1_ffn_in['b1'], 'L1_ffn_W2': _L1_ffn_in['W2'], 'L1_ffn_b2': _L1_ffn_in['b2']}

def reference(x, adj, L0_gnn_w1_loop, L0_gnn_w1_neigh, L0_gnn_b1, L0_gnn_w2_loop, L0_gnn_w2_neigh, L0_gnn_b2, L0_ffn_router_w1, L0_ffn_router_b1, L0_ffn_router_w2, L0_ffn_router_b2, L0_ffn_expert_w1, L0_ffn_expert_b1, L0_ffn_expert_w2, L0_ffn_expert_b2, L0_ffn_expert_w3, L0_ffn_expert_b3, L1_gnn_node_vec1, L1_gnn_node_vec2, L1_gnn_W, L1_gnn_b, L1_ffn_Wr, L1_ffn_br, L1_ffn_ln_g, L1_ffn_ln_b, L1_ffn_W1, L1_ffn_b1, L1_ffn_W2, L1_ffn_b2):
    import jax
    import jax.numpy as jnp

    def _L0_gnn_ref(x, adj, w1_loop, w1_neigh, b1, w2_loop, w2_neigh, b2):
        import jax, jax.numpy as jnp
        import numpy as np
        N = 3445
        B = 32
        IN_DIM = 128
        HID_DIM = 128

        def _make_adj(key):
            a = jax.random.uniform(key, (N, N), dtype=jnp.float32)
            a = (a < 0.001).astype(jnp.float32)
            a = jnp.maximum(a, a.T)
            deg = jnp.sum(a, axis=1, keepdims=True)
            return a / jnp.maximum(deg, 1.0)

        def _graph_conv(x, adj, w_loop, w_neigh, b):
            loop = jnp.einsum('bnd,dh->bnh', x, w_loop)
            neigh = jnp.einsum('nm,bmh->bnh', adj, jnp.einsum('bnd,dh->bnh', x, w_neigh))
            return loop + neigh + b
        h = jax.nn.relu(_graph_conv(x, adj, w1_loop, w1_neigh, b1))
        h = jax.nn.relu(_graph_conv(h, adj, w2_loop, w2_neigh, b2))
        return (x + h) * 0.5

    def _L0_ffn_ref(features, router_w1, router_b1, router_w2, router_b2, expert_w1, expert_b1, expert_w2, expert_b2, expert_w3, expert_b3):
        import jax, jax.numpy as jnp
        import numpy as np
        E, D, H, TOP_K = (6, 128, 128, 2)
        ROUTER_H = D // 2
        rh = jax.nn.relu(features @ router_w1 + router_b1)
        expert_logits = jax.nn.softmax(rh @ router_w2 + router_b2, axis=-1)
        top_w, top_i = jax.lax.top_k(expert_logits, TOP_K)
        routing_weights = jax.nn.softmax(top_w, axis=-1)
        h1 = jax.nn.relu(jnp.einsum('bsd,edh->bseh', features, expert_w1) + expert_b1)
        h2 = jax.nn.relu(jnp.einsum('bseh,ehf->bsef', h1, expert_w2) + expert_b2)
        expert_out = jnp.einsum('bsef,efo->bseo', h2, expert_w3) + expert_b3
        sel = jnp.take_along_axis(expert_out, top_i[:, :, :, None], axis=2)
        combined = jnp.sum(sel * routing_weights[..., None], axis=2)
        return combined

    def _L1_gnn_ref(x, support0, support1, node_vec1, node_vec2, W, b):
        import jax, jax.numpy as jnp
        import numpy as np
        B, N, H, OUT, RANK = (64, 512, 128, 128, 10)
        ORDER = 2

        def _conv(x, adj):
            return x * jnp.sum(adj, axis=1)[None, :, None]
        adaptive = jax.nn.softmax(jax.nn.relu(node_vec1 @ node_vec2), axis=1)
        outputs = [x]
        for adj in (support0, support1, adaptive):
            x1 = _conv(x, adj)
            outputs.append(x1)
            for _ in range(2, ORDER + 1):
                x1 = _conv(x1, adj)
                outputs.append(x1)
        out = jnp.concatenate(outputs, axis=2)
        out = out @ W + b
        return out

    def _L1_ffn_ref(x, Wr, br, ln_g, ln_b, W1, b1, W2, b2):
        import jax, jax.numpy as jnp
        import numpy as np
        TOP_K = 2
        LN_EPS = 1e-05
        B, S, D = x.shape
        N = B * S
        xt = x.reshape(N, D)
        logits = xt @ Wr + br
        probs = jax.nn.softmax(logits, axis=-1)
        top_p, top_idx = jax.lax.top_k(probs, TOP_K)
        weights = top_p / top_p.sum(axis=-1, keepdims=True)
        mu = xt.mean(axis=-1, keepdims=True)
        var = ((xt - mu) ** 2).mean(axis=-1, keepdims=True)
        xn = (xt - mu) * jax.lax.rsqrt(var + LN_EPS)
        xe = xn[None, :, :] * ln_g[:, None, :] + ln_b[:, None, :]
        h = jax.nn.gelu(jnp.einsum('end,edh->enh', xe, W1) + b1[:, None, :], approximate=False)
        y = jnp.einsum('enh,ehd->end', h, W2) + b2[:, None, :]
        y_tok = jnp.transpose(y, (1, 0, 2))
        sel = jnp.take_along_axis(y_tok, top_idx[:, :, None], axis=1)
        out = (weights[:, :, None] * sel).sum(axis=1)
        return out.reshape(B, S, D)
    x = x + _L0_gnn_ref(_layernorm(x, axis=-1), adj, L0_gnn_w1_loop, L0_gnn_w1_neigh, L0_gnn_b1, L0_gnn_w2_loop, L0_gnn_w2_neigh, L0_gnn_b2)
    x = x + _L0_ffn_ref(_layernorm(x, axis=-1), L0_ffn_router_w1, L0_ffn_router_b1, L0_ffn_router_w2, L0_ffn_router_b2, L0_ffn_expert_w1, L0_ffn_expert_b1, L0_ffn_expert_w2, L0_ffn_expert_b2, L0_ffn_expert_w3, L0_ffn_expert_b3)
    x = x + _L1_gnn_ref(_layernorm(x, axis=-1), adj, adj, L1_gnn_node_vec1, L1_gnn_node_vec2, L1_gnn_W, L1_gnn_b)
    x = x + _L1_ffn_ref(_layernorm(x, axis=-1), L1_ffn_Wr, L1_ffn_br, L1_ffn_ln_g, L1_ffn_ln_b, L1_ffn_W1, L1_ffn_b1, L1_ffn_W2, L1_ffn_b2)
    return x

_drawn_inputs = setup_inputs


def setup_inputs(seed=0):
    import zlib

    import numpy as np

    out = dict(_drawn_inputs(seed))
    spreads = {'L0_gnn_b1': (0.0, 0.1),
     'L0_gnn_b2': (0.0, 0.1),
     'L0_ffn_router_b1': (0.0, 0.1),
     'L0_ffn_router_b2': (0.0, 0.1),
     'L0_ffn_expert_b1': (0.0, 0.424),
     'L0_ffn_expert_b2': (0.0, 0.1),
     'L0_ffn_expert_b3': (0.0, 0.1),
     'L1_gnn_b': (0.0, 0.1),
     'L1_ffn_br': (0.0, 0.1),
     'L1_ffn_ln_g': (1.0, 0.2),
     'L1_ffn_ln_b': (0.0, 0.298),
     'L1_ffn_b1': (0.0, 0.293),
     'L1_ffn_b2': (0.0, 0.1)}
    factors = {'L1_gnn_node_vec1': 200.0, 'L1_gnn_node_vec2': 200.0}
    for name, (base, spread) in spreads.items():
        noise = np.random.default_rng([zlib.crc32(name.encode()), seed]).standard_normal(out[name].shape)
        drawn = base * np.exp(spread * noise) if base else spread * noise
        out[name] = jnp.asarray(drawn.astype(out[name].dtype))
    for name, factor in factors.items():
        out[name] = (out[name] * factor).astype(out[name].dtype)
    return out
```

```python
from contextlib import ExitStack

import concourse.bass as bass
from concourse import mybir

P = 128
F32 = mybir.dt.float32
U32 = mybir.dt.uint32
ALU = mybir.AluOpType
ACT = mybir.ActivationFunctionType
AX = mybir.AxisListType
LN_EPS = 1e-5
PAD_LOGIT = -1e30
PER_PASS = 110


class Steps:

    def __init__(self, eng, sem):
        self.eng, self.sem, self.n = eng, sem, 0

    def add(self, ins):
        ins.then_inc(self.sem, 1)
        self.n += 1

    def wait(self):
        self.eng.wait_ge(self.sem, self.n)

    def clear(self):
        if self.n:
            self.wait()
        self.eng.sem_clear(self.sem)
        self.n = 0


def program(nc, x, adjT, w1_loop, w1_neigh, b1, w2_loop, w2_neigh, b2, rw1, rb1, rw2, rb2, ew1, eb1, ew2, eb2,
            ew3, eb3, nv1T, nv2, gW, gb, Wr, br, lngT, lnbT, W1, b1T, W2, b2e, out):
    B, N, D = x.shape
    T = B * N
    NT = N // P
    G = T // N
    GW = NT * D
    EB = ew1.shape[0]
    RH = rw1.shape[1]
    ED = W1.shape[0]
    H = W1.shape[2]
    HC = H // P
    RANK = nv1T.shape[0]
    QB = 4

    ctx = ExitStack()
    with ctx:
        def sb(name, shape, dt=F32):
            return ctx.enter_context(nc.sbuf_tensor(name, shape, dt))

        def ps(name, shape):
            return ctx.enter_context(nc.psum_tensor(name, shape, F32))

        def sem(name):
            return ctx.enter_context(nc.semaphore(name))

        xs = sb("xs", [P, G * GW])
        big = sb("big", [P, G * GW])
        fA = big[:, 0:2 * QB * GW].rearrange("p (h b n) -> p h b n", h=2, b=QB)
        adp = big[:, 8 * GW:8 * GW + NT * N].rearrange("p (c n) -> p c n", c=NT)
        dia = big[:, 12 * GW:12 * GW + NT * P].rearrange("p (c n) -> p c n", c=NT)
        adjT_sb = sb("adjT_sb", [P, NT, N])
        wA = sb("wA", [P, 4, D])
        b1_sb = sb("b1_sb", [P, 1])
        b2_bc = sb("b2_bc", [P, QB, D])
        rw1_sb = sb("rw1_sb", [P, RH])
        rb1_sb = sb("rb1_sb", [RH, 1])
        rw2_sb = sb("rw2_sb", [RH, EB])
        rb2_bc = sb("rb2_bc", [P, NT, EB])
        ew1_sb = sb("ew1_sb", [P, EB, D])
        ew2_sb = sb("ew2_sb", [P, EB, D])
        ew3_sb = sb("ew3_sb", [P, EB, D])
        eb1_sb = sb("eb1_sb", [P, EB])
        eb2_sb = sb("eb2_sb", [P, EB])
        eb3_sb = sb("eb3_sb", [EB, D])
        nv1T_sb = sb("nv1T_sb", [RANK, N])
        nv2_sb = sb("nv2_sb", [RANK, N])
        gW_sb = sb("gW_sb", [P, 7, D])
        gb_bc = sb("gb_bc", [P, NT, D])
        Wr_sb = sb("Wr_sb", [P, ED])
        br_bc = sb("br_bc", [P, NT, ED])
        lngT_sb = sb("lngT_sb", [P, ED])
        lnbT_sb = sb("lnbT_sb", [P, ED])
        W1_sb = sb("W1_sb", [P, ED, H])
        b1T_sb = sb("b1T_sb", [P, ED * HC])
        W2_sb = sb("W2_sb", [P, ED, HC, D])
        b2e_sb = sb("b2e_sb", [ED, D])
        ident = sb("ident", [P, P])
        ones = sb("ones", [P, P])
        iota8 = sb("iota8", [P, NT, 8])
        eps = sb("eps", [P, QB * NT])
        neg_half = sb("neg_half", [P, QB * NT])
        s1_bc = sb("s1_bc", [P, N])
        s2_bc = sb("s2_bc", [P, N])
        a1_bc = sb("a1_bc", [P, N])
        a2_bc = sb("a2_bc", [P, N])
        adm = sb("adm", [P, 4, NT])
        st = [sb(f"st{k}", [P, NT, 6]) for k in range(4)]
        mv = [sb(f"mv{k}", [P, NT, 2]) for k in range(4)]
        ve = [sb(f"ve{k}", [P, NT]) for k in range(4)]
        rs = [sb(f"rs{k}", [P, NT]) for k in range(4)]
        ft = [sb(f"ft{k}", [P, NT, D]) for k in range(4)]
        fT = [sb(f"fT{k}", [P, N]) for k in range(3)]
        stA = sb("stA", [P, QB * NT, 6])
        mvA = sb("mvA", [P, QB * NT, 2])
        veA = sb("veA", [P, QB * NT])
        rsA = sb("rsA", [P, QB * NT])
        uT = sb("uT", [P, 2, N])
        fTA = sb("fTA", [P, 2, N])
        hT = sb("hT", [P, 2, HC, N])
        h1A = hT[:, 0]
        gA = hT[:, 1].rearrange("p m (b d) -> p m b d", b=QB)
        rhT = sb("rhT", [RH, N])
        h1T = sb("h1T", [P, 2, N])
        h2T = sb("h2T", [P, 2, N])
        fs = sb("fs", [P, 4, N])
        lg = [sb(f"lg{k}", [P, NT, 8]) for k in range(2)]
        mx = [sb(f"mx{k}", [P, NT, 8]) for k in range(2)]
        ix = [sb(f"ix{k}", [P, NT, 8], U32) for k in range(2)]
        ixf = [sb(f"ixf{k}", [P, 2, NT]) for k in range(2)]
        oh = [sb(f"oh{k}", [P, 2, NT, 8]) for k in range(2)]
        dl = [sb(f"dl{k}", [P, NT, 8]) for k in range(2)]
        ex = [sb(f"ex{k}", [P, NT, 8]) for k in range(2)]
        wt = [sb(f"wt{k}", [P, 8, NT]) for k in range(2)]
        cB = sb("cB", [P, NT, 8])
        cD = sb("cD", [P, G, NT, 8])
        cDs = sb("cDs", [P, NT, 8])
        cT = sb("cT", [8, N])
        cTD = sb("cTD", [8, N])

        bank = [ps(f"bank{k}", [P, 512]) for k in range(8)]

        x_in = [sem(f"x_in{q}") for q in range(4)]
        w_in = sem("w_in")
        x_out = sem("x_out")
        pool_step = sem("pool_step")
        dve_step = sem("dve_step")
        act_step = sem("act_step")
        consts = sem("consts")
        prep_pe = sem("prep_pe")
        prep_dve = sem("prep_dve")
        prep_act = sem("prep_act")
        ln_stats = [sem(f"ln_stats{k}") for k in range(4)]
        ln_rstd = [sem(f"ln_rstd{k}") for k in range(4)]
        ln_f = [sem(f"ln_f{k}") for k in range(4)]
        turned = [sem(f"turned{k}") for k in range(4)]
        turned_sb = [sem(f"turned_sb{k}") for k in range(4)]
        aln_stats, aln_rstd, aln_f = sem("aln_stats"), sem("aln_rstd"), sem("aln_f")
        a_fp, a_fT, a_up, a_uT, a_hp, a_h, a_gp, a_g, a_z, a_zfree = [
            sem("a_" + s) for s in "fp fT up uT hp h gp g z zfree".split()]
        b_rp, b_rh, b_lp, b_lfree, b_hp, b_h, b_op, b_ofree, b_c, b_cp, b_cT, b_bias, b_biasfree, b_ask, b_exp = [
            sem("b_" + s) for s in "rp rh lp lfree hp h op ofree c cp cT bias biasfree ask exp".split()]
        c_fs, c_p, c_free, c_b = [sem("c_" + s) for s in "fs p free b".split()]
        d_lp, d_lfree, d_ask, d_exp, d_xn, d_c = [sem("d_" + s) for s in "lp lfree ask exp xn c".split()]
        e_hp, e_h, e_yp, e_yfree, e_cs, e_cp, e_cT, e_bias, x_done = [
            sem("e_" + s) for s in "hp h yp yfree cs cp cT bias xdone".split()]

        xr = x.rearrange("b (c p) d -> p b c d", p=P)
        xs_v = xs[:, :].rearrange("p (b c d) -> p b c d", b=B, c=NT)

        loads = [
            (adjT_sb[:, :, :], adjT.rearrange("(c p) n -> p c n", p=P)),
            (wA[:, 0, :], w1_loop), (wA[:, 1, :], w1_neigh), (wA[:, 2, :], w2_loop), (wA[:, 3, :], w2_neigh),
            (b1_sb[:, :], b1), (b2_bc[:, :, :], b2),
            (rw1_sb[:, :], rw1), (rb1_sb[:, :], rb1), (rw2_sb[:, :], rw2),
            (rb2_bc[:, :, :], rb2),
            (ew1_sb[:, :, :], ew1.rearrange("e d h -> d e h")),
            (ew2_sb[:, :, :], ew2.rearrange("e d h -> d e h")),
            (ew3_sb[:, :, :], ew3.rearrange("e d h -> d e h")),
            (eb1_sb[:, :], eb1), (eb2_sb[:, :], eb2), (eb3_sb[:, :], eb3),
            (nv1T_sb[:, :], nv1T), (nv2_sb[:, :], nv2),
            (gW_sb[:, :, :], gW.rearrange("(k p) n -> p k n", p=P)),
            (gb_bc[:, :, :], gb),
            (Wr_sb[:, :], Wr), (br_bc[:, :, :], br),
            (lngT_sb[:, :], lngT), (lnbT_sb[:, :], lnbT),
            (W1_sb[:, :, :], W1.rearrange("e d h -> d e h")),
            (b1T_sb[:, :], b1T),
            (W2_sb[:, :, :, :], W2.rearrange("e (c p) d -> p e c d", p=P)),
            (b2e_sb[:, :], b2e),
        ]
        W_IN = 16 * len(loads)

        HID = [(1, 0), (1, 1), (2, 0), (1, 2), (2, 1), (1, 3), (2, 2), (1, 4), (2, 3), (1, 5), (2, 4), (2, 5)]
        NH = len(HID)

        block = ctx.enter_context(nc.Block())

        def grp(t, g, w=GW):
            return t[:, bass.ds(g * w, w)]

        def pipeline(eng, body, steps=None):
            body(0, True, False, True)
            if steps:
                steps.clear()
            with eng.Fori(1, G - 1) as n:
                body(n, True, True, True)
                if steps:
                    steps.clear()
            body(G - 1, True, True, False)
            body(G, False, True, False)

        @block.sync
        def _(sp):
            for q in range(4):
                sp.dma_start(xs_v[:, QB * q:QB * q + QB], xr[:, QB * q:QB * q + QB]).then_inc(x_in[q], 16)
            for dst, src in loads:
                sp.dma_start(dst, src).then_inc(w_in, 16)
            with sp.Fori(0, G) as g:
                sp.wait_ge(x_done, g + 1)
                sp.dma_start(out[bass.ds(g, 1)].rearrange("b (c p) d -> p (b c) d", p=P),
                             grp(xs, g).rearrange("p (c d) -> p c d", c=NT)).then_inc(x_out, 16)
            sp.wait_ge(x_out, 16 * G)

        @block.gpsimd
        def _(pool):
            step = Steps(pool, pool_step)
            step.add(pool.memset(ident[:, :], 0.0))
            pool.memset(ones[:, :], 1.0).then_inc(consts, 1)
            pool.memset(neg_half[:, :], -0.5).then_inc(consts, 1)
            pool.memset(eps[:, :], LN_EPS).then_inc(consts, 1)
            for k in range(2):
                pool.memset(lg[k][:, :, :], PAD_LOGIT).then_inc(consts, 1)
            pool.iota(iota8[:, :, :], [[0, NT], [1, 8]], channel_multiplier=0,
                      allow_small_or_imprecise_dtypes=True).then_inc(consts, 1)
            step.wait()
            pool.affine_select(out=ident[:, :], in_=ident[:, :], compare_op=ALU.not_equal, fill=1.0, base=0,
                               pattern=[[-1, P]], channel_multiplier=1).then_inc(consts, 1)
            pool.wait_ge(consts, 7)

            step.clear()
            with pool.Fori(0, B // QB) as q:
                pool.wait_ge(aln_stats, q + 1)
                step.add(pool.tensor_tensor(veA[:, :], mvA[:, :, 1], eps[:, :], ALU.add))
                step.wait()
                pool.tensor_tensor(rsA[:, :], veA[:, :], neg_half[:, :], ALU.pow).then_inc(aln_rstd, 1)
                step.clear()

            def rstd(k, n):
                pool.wait_ge(ln_stats[k], n)
                step.add(pool.tensor_tensor(ve[k][:, :], mv[k][:, :, 1], eps[:, 0:NT], ALU.add))
                step.wait()
                pool.tensor_tensor(rs[k][:, :], ve[k][:, :], neg_half[:, 0:NT], ALU.pow).then_inc(ln_rstd[k], 1)

            def body(n, cur, prev, nxt):
                if prev:
                    rstd(1, n)
                    pool.wait_ge(ln_f[1], n)
                    pool.tensor_tensor(grp(xs, n - 1), grp(xs, n - 1), gb_bc[:, :, :].rearrange("p a b -> p (a b)"),
                                       ALU.add).then_inc(c_b, 1)
                    pool.wait_ge(turned_sb[1], n)
                    for k, by in enumerate((s1_bc, s2_bc, a1_bc, a2_bc)):
                        pool.tensor_tensor(fs[:, k, :], fT[1][:, :], by[:, :], ALU.mult).then_inc(c_fs, 1)
                    rstd(2, n)
                    rstd(3, n)
                if nxt:
                    rstd(0, n + 2)

            pool.wait_ge(prep_dve, 4)
            rstd(0, 1)
            pipeline(pool, body, step)

        @block.tensor
        def _(pe):
            mm = pe.matmul
            pe.wait_ge(consts, 7)
            pe.wait_ge(w_in, W_IN)
            for m in range(NT):
                ins = mm(bank[0][:, :], ones[:, :], adjT_sb[:, m, :], start=(m == 0), stop=(m == NT - 1))
            ins.then_inc(prep_pe, 1)
            for c in range(NT):
                ins = mm(bank[1 + c][:, :], nv1T_sb[:, c * P:(c + 1) * P], nv2_sb[:, :], start=True, stop=True)
            ins.then_inc(prep_pe, 1)
            for e in range(ED):
                for c in range(HC):
                    k = e * HC + c
                    ins = mm(bank[5][:, k:k + 1], W1_sb[:, e, c * P:(c + 1) * P], lnbT_sb[:, e:e + 1],
                             start=True, stop=True)
            ins.then_inc(prep_pe, 1)
            pe.wait_ge(prep_dve, 3)
            for c in range(NT):
                ins = mm(bank[6][:, c * P:(c + 1) * P], ones[:, :], dia[:, c, :], start=True, stop=True)
            ins.then_inc(prep_pe, 1)
            pe.wait_ge(prep_dve, 4)

            def first_layer(q, half, i):
                f = fA[:, half]
                done = q * QB

                def turn(b):
                    if b == 0:
                        pe.wait_ge(aln_f, q + 1)
                    if b > 0:
                        pe.wait_ge(a_fT, done + b)
                    for c in range(NT):
                        ins = pe.transpose(bank[0][:, c * P:(c + 1) * P], f[:, b, c * D:(c + 1) * D], ident[:, :])
                    ins.then_inc(a_fp, 1)

                def neigh(b):
                    if b > 0:
                        pe.wait_ge(a_uT, done + b)
                    for m in range(NT):
                        ins = mm(bank[1][:, :], f[:, b, m * D:(m + 1) * D], adjT_sb[:, m, :],
                                 start=(m == 0), stop=(m == NT - 1))
                    ins.then_inc(a_up, 1)

                def hidden(b):
                    pe.wait_ge(a_fT, done + b + 1)
                    pe.wait_ge(a_uT, done + b + 1)
                    if b > 0:
                        pe.wait_ge(a_h, done + b)
                    mm(bank[2][:, :], wA[:, 0, :], fTA[:, b % 2, :], start=True, stop=False)
                    mm(bank[2][:, :], wA[:, 1, :], uT[:, b % 2, :], start=False, stop=True).then_inc(a_hp, 1)

                def second(b):
                    pe.wait_ge(a_h, done + b + 1)
                    if b > 0:
                        pe.wait_ge(a_g, done + b)
                    for m in range(NT):
                        ins = mm(bank[3][:, m * D:(m + 1) * D], h1A[:, b, m * P:(m + 1) * P], wA[:, 3, :],
                                 start=True, stop=True)
                    ins.then_inc(a_gp, 1)

                turn(0)
                neigh(0)
                turn(1)
                hidden(0)
                neigh(1)
                turn(2)
                hidden(1)
                second(0)
                neigh(2)
                turn(3)
                hidden(2)
                second(1)
                neigh(3)
                second(2)
                hidden(3)
                second(3)
                pe.wait_ge(a_g, done + QB)
                for c in range(NT):
                    pe.wait_ge(a_zfree, q * NT + (c + 1))
                    z = bank[4 + c % 2]
                    for m in range(NT):
                        mm(z[:, :], adjT_sb[:, m, c * P:(c + 1) * P], gA[:, m, :, :], start=(m == 0), stop=(m == NT - 1))
                    for b in range(QB):
                        ins = mm(z[:, b * D:(b + 1) * D], h1A[:, b, c * P:(c + 1) * P], wA[:, 2, :],
                                 start=False, stop=True, skip_group_check=True)
                    ins.then_inc(a_z, 1)

            with pe.Fori(0, B // QB // 2) as i:
                for half in range(2):
                    first_layer(i * 2 + half, half, i)

            def turn(k, n, bank_free=None):
                if bank_free:
                    pe.wait_ge(*bank_free)
                pe.wait_ge(ln_f[k], n)
                for c in range(NT):
                    ins = pe.transpose(bank[0][:, c * P:(c + 1) * P], ft[k][:, c, :], ident[:, :])
                ins.then_inc(turned[k], 1)

            def hid(n, j):
                layer, e = HID[j]
                if layer == 2:
                    pe.wait_ge(b_h, n * NH + (HID.index((1, e)) + 1))
                if not (isinstance(n, int) and n == 0 and j < 2):
                    pe.wait_ge(b_h, n * NH + (j - 1))
                w, f = (ew1_sb, fT[0][:, :]) if layer == 1 else (ew2_sb, h1T[:, e % 2, :])
                mm(bank[3 + j % 2][:, :], w[:, e, :], f, start=True, stop=True).then_inc(b_hp, 1)

            def outp(n, e):
                pe.wait_ge(b_h, n * NH + (HID.index((2, e)) + 1))
                if not (isinstance(n, int) and n == 0 and e < 2):
                    pe.wait_ge(b_ofree, n * EB + (e - 1))
                for c in range(NT):
                    ins = mm(bank[5 + e % 2][:, c * D:(c + 1) * D], h2T[:, e % 2, c * P:(c + 1) * P], ew3_sb[:, e, :],
                             start=True, stop=True)
                ins.then_inc(b_op, 1)

            def body(n, cur, prev, nxt):
                if cur:
                    turn(0, n + 1, (d_xn, n) if prev else None)
                    pe.wait_ge(turned_sb[0], n + 1)
                    mm(bank[1][0:RH, :], rw1_sb[:, :], fT[0][:, :], start=True, stop=True).then_inc(b_rp, 1)
                    hid(n, 0)
                    hid(n, 1)
                    pe.wait_ge(b_rh, n + 1)
                    for c in range(NT):
                        ins = mm(bank[2][:, c * EB:(c + 1) * EB], rhT[:, c * P:(c + 1) * P], rw2_sb[:, :],
                                 start=True, stop=True)
                    ins.then_inc(b_lp, 1)
                    hid(n, 2)
                if prev:
                    turn(1, n, None if cur else (d_xn, n))
                if cur:
                    hid(n, 3)
                    hid(n, 4)
                    outp(n, 0)
                if prev:
                    pe.wait_ge(c_fs, n * 4)
                    for c in range(NT):
                        for k in range(5):
                            f = fT[1][:, c * P:(c + 1) * P] if k == 0 else fs[:, k - 1, c * P:(c + 1) * P]
                            w = gW_sb[:, k if k < 3 else k + 2, :]
                            ins = mm(bank[7][:, c * D:(c + 1) * D], f, w, start=(k == 0), stop=(k == 4))
                    ins.then_inc(c_p, 1)
                if cur:
                    hid(n, 5)
                    hid(n, 6)
                    outp(n, 1)
                    pe.wait_ge(b_c, n + 1)
                    for c in range(NT):
                        ins = pe.transpose(bank[1][0:8, c * P:(c + 1) * P], cB[:, c, :], ident[:, :])
                    ins.then_inc(b_cp, 1)
                if cur:
                    hid(n, 7)
                    hid(n, 8)
                    outp(n, 2)
                    pe.wait_ge(b_cT, n + 1)
                    for c in range(NT):
                        ins = mm(bank[1][:, c * D:(c + 1) * D], cT[0:EB, c * P:(c + 1) * P], eb3_sb[:, :],
                                 start=True, stop=True)
                    ins.then_inc(b_bias, 1)
                if prev:
                    turn(2, n, (turned_sb[1], n))
                if cur:
                    hid(n, 9)
                    hid(n, 10)
                    outp(n, 3)
                if prev:
                    pe.wait_ge(turned_sb[2], n)
                    for c in range(NT):
                        ins = mm(bank[2][:, c * ED:(c + 1) * ED], fT[2][:, c * P:(c + 1) * P], Wr_sb[:, :],
                                 start=True, stop=True)
                    ins.then_inc(d_lp, 1)
                if cur:
                    hid(n, 11)
                    outp(n, 4)
                if prev:
                    turn(3, n)
                if cur:
                    outp(n, 5)

            pe.wait_ge(a_zfree, G + 2)
            pipeline(pe, body)

            with pe.Fori(0, G) as g:
                xn = grp(big, g)

                def hid2(e):
                    for c in range(HC):
                        u = e * HC + c
                        if u == 0:
                            pe.wait_ge(d_xn, G + 1)
                        if u >= 2:
                            pe.wait_ge(e_h, g * (ED * HC) + (u - 1))
                        mm(bank[u % 2][:, :], W1_sb[:, e, c * P:(c + 1) * P], xn, start=True, stop=True).then_inc(e_hp, 1)

                def out2(e):
                    pe.wait_ge(e_h, g * (ED * HC) + (e + 1) * HC)
                    if e >= 2:
                        pe.wait_ge(e_yfree, g * ED + (e - 1))
                    for c in range(NT):
                        for k in range(HC):
                            ins = mm(bank[2 + e % 2][:, c * D:(c + 1) * D], hT[:, e % 2, k, c * P:(c + 1) * P],
                                     W2_sb[:, e, k, :], start=(k == 0), stop=(k == HC - 1))
                    ins.then_inc(e_yp, 1)

                pe.wait_ge(e_cs, g + 1)
                for c in range(NT):
                    ins = pe.transpose(bank[4][0:8, c * P:(c + 1) * P], cDs[:, c, :], ident[:, :])
                ins.then_inc(e_cp, 1)
                hid2(0)
                pe.wait_ge(e_cT, g + 1)
                for c in range(NT):
                    ins = mm(bank[5][:, c * D:(c + 1) * D], cTD[:, c * P:(c + 1) * P], b2e_sb[:, :],
                             start=True, stop=True)
                ins.then_inc(e_bias, 1)
                for e in range(ED):
                    if e + 1 < ED:
                        hid2(e + 1)
                    out2(e)

        @block.scalar
        def _(act):
            step = Steps(act, act_step)
            act.wait_ge(prep_dve, 2)
            for c in range(NT):
                ins = act.activation(adp[:, c, :], adp[:, c, :], ACT.Exp, bias=adm[:, 0, c:c + 1])
                ins.then_inc(prep_act, 1)

            act.wait_ge(prep_dve, 4)

            def first_layer(q):
                done = q * QB

                def copies(b):
                    act.wait_ge(a_fp, done + b + 1)
                    if b >= 2:
                        act.wait_ge(a_hp, done + b - 1)
                    act.copy(fTA[:, b % 2, :], bank[0][:, :]).then_inc(a_fT, 1)

                def copies2(b):
                    act.wait_ge(a_up, done + b + 1)
                    act.copy(uT[:, b % 2, :], bank[1][:, :]).then_inc(a_uT, 1)

                def relu(b):
                    act.wait_ge(a_hp, done + b + 1)
                    act.activation(h1A[:, b, :], bank[2][:, :], ACT.Relu, bias=b1_sb[:, :]).then_inc(a_h, 1)

                def second(b):
                    act.wait_ge(a_gp, done + b + 1)
                    act.copy(gA[:, :, b, :], bank[3][:, :].rearrange("p (m d) -> p m d", m=NT)).then_inc(a_g, 1)

                copies(0)
                copies2(0)
                copies(1)
                relu(0)
                copies2(1)
                copies(2)
                relu(1)
                second(0)
                copies2(2)
                copies(3)
                relu(2)
                second(1)
                copies2(3)
                second(2)
                relu(3)
                second(3)

            with act.Fori(0, B // QB) as q:
                first_layer(q)

            def turned_copy(k, n):
                act.wait_ge(turned[k], n)
                if k < 3:
                    act.copy(fT[k][:, :], bank[0][:, :]).then_inc(turned_sb[k], 1)
                else:
                    act.copy(grp(big, n - 1), bank[0][:, :]).then_inc(d_xn, 1)

            def hid(n, j):
                layer, e = HID[j]
                act.wait_ge(b_hp, n * NH + (j + 1))
                if e >= 2 and layer == 1:
                    act.wait_ge(b_hp, n * NH + (HID.index((2, e - 2)) + 1))
                if e >= 2 and layer == 2:
                    act.wait_ge(b_op, n * EB + (e - 1))
                dst, b = (h1T, eb1_sb) if layer == 1 else (h2T, eb2_sb)
                act.activation(dst[:, e % 2, :], bank[3 + j % 2][:, :], ACT.Relu, bias=b[:, e:e + 1]).then_inc(b_h, 1)

            def body(n, cur, prev, nxt):
                if cur:
                    turned_copy(0, n + 1)
                    act.wait_ge(b_rp, n + 1)
                    act.activation(rhT[:, :], bank[1][0:RH, :], ACT.Relu, bias=rb1_sb[:, :]).then_inc(b_rh, 1)
                    hid(n, 0)
                    hid(n, 1)
                    hid(n, 2)
                if prev:
                    turned_copy(1, n)
                if cur:
                    act.wait_ge(b_ask, n * 2 + 1)
                    act.activation(ex[0][:, :, :], dl[0][:, :, :], ACT.Exp).then_inc(b_exp, 1)
                    hid(n, 3)
                    hid(n, 4)
                    act.wait_ge(b_ask, n * 2 + 2)
                    act.activation(wt[0][:, 4, :], wt[0][:, 3, :], ACT.Exp).then_inc(b_exp, 1)
                    hid(n, 5)
                    hid(n, 6)
                    act.wait_ge(b_cp, n + 1)
                    act.copy(cT[:, :], bank[1][0:8, :]).then_inc(b_cT, 1)
                if cur:
                    hid(n, 7)
                    hid(n, 8)
                if prev:
                    turned_copy(2, n)
                if cur:
                    hid(n, 9)
                    hid(n, 10)
                    hid(n, 11)
                if prev:
                    act.wait_ge(d_ask, n)
                    act.activation(wt[1][:, 1, :], wt[1][:, 0, :], ACT.Exp).then_inc(d_exp, 1)
                    turned_copy(3, n)

            act.sem_inc(d_xn, 1)
            pipeline(act, body)

            with act.Fori(0, G) as g:
                act.wait_ge(e_cp, g + 1)
                act.copy(cTD[:, :], bank[4][0:8, :]).then_inc(e_cT, 1)
                for e in range(ED):
                    for c in range(HC):
                        u = e * HC + c
                        act.wait_ge(e_hp, g * (ED * HC) + (u + 1))
                        if c == 0 and e >= 2:
                            act.wait_ge(e_yp, g * ED + (e - 1))
                        act.activation(hT[:, e % 2, c, :], bank[u % 2][:, :], ACT.Gelu,
                                       bias=b1T_sb[:, u:u + 1]).then_inc(e_h, 1)

        @block.vector
        def _(dve):
            step = Steps(dve, dve_step)

            def dep(ins):
                step.add(ins)
                step.wait()

            dve.sem_inc(a_zfree, 2)
            dve.wait_ge(consts, 7)
            dve.wait_ge(w_in, W_IN)
            step.add(dve.tensor_tensor(gW_sb[:, 1, :], gW_sb[:, 1, :], gW_sb[:, 3, :], ALU.add))
            step.add(dve.tensor_tensor(gW_sb[:, 2, :], gW_sb[:, 2, :], gW_sb[:, 4, :], ALU.add))
            dve.wait_ge(prep_pe, 1)
            dep(dve.tensor_copy(s1_bc[:, :], bank[0][:, :]))
            dep(dve.tensor_tensor(s2_bc[:, :], s1_bc[:, :], s1_bc[:, :], ALU.mult))
            dve.wait_ge(prep_pe, 2)
            for c in range(NT):
                ins = dve.tensor_scalar(adp[:, c, :], bank[1 + c][:, :], 0.0, None, ALU.max)
                step.add(ins)
            step.wait()
            for c in range(NT):
                ins = dve.tensor_reduce(adm[:, 0, c:c + 1], adp[:, c, :], AX.X, ALU.max, negate=True)
                step.add(ins)
            step.wait()
            dve.sem_inc(prep_dve, 2)
            dve.wait_ge(prep_act, NT)
            for c in range(NT):
                step.add(dve.tensor_reduce(adm[:, 1, c:c + 1], adp[:, c, :], AX.X, ALU.add))
            step.wait()
            dep(dve.reciprocal(adm[:, 2, :], adm[:, 1, :]))
            for c in range(NT):
                step.add(dve.tensor_scalar(adp[:, c, :], adp[:, c, :], adm[:, 2, c:c + 1], None, ALU.mult))
            step.wait()
            for c in range(NT):
                step.add(dve.tensor_reduce(adm[:, 3, c:c + 1], adp[:, c, :], AX.X, ALU.add))
            step.wait()
            for c in range(NT):
                step.add(dve.tensor_scalar(dia[:, c, :], ident[:, :], adm[:, 3, c:c + 1], None, ALU.mult))
            step.wait()
            dve.sem_inc(prep_dve, 1)
            dve.wait_ge(prep_pe, 4)
            dep(dve.tensor_copy(a1_bc[:, :], bank[6][:, :]))
            dep(dve.tensor_tensor(a2_bc[:, :], a1_bc[:, :], a1_bc[:, :], ALU.mult))
            step.add(dve.tensor_tensor(b1T_sb[:, :], b1T_sb[:, :], bank[5][:, 0:ED * HC], ALU.add))
            for e in range(ED):
                step.add(dve.tensor_scalar(W1_sb[:, e, :], W1_sb[:, e, :], lngT_sb[:, e:e + 1], None, ALU.mult))
            step.wait()
            dve.sem_inc(prep_dve, 1)

            def norm_stats(q):
                for t in range(QB * NT):
                    step.add(dve.bn_stats(stA[:, t, :], xs[:, bass.ds(q * (QB * GW) + t * D, D)]))
                step.wait()
                for t in range(QB * NT):
                    ins = dve.bn_aggr(mvA[:, t, :], stA[:, t, :])
                    if t < QB * NT - 1:
                        step.add(ins)
                ins.then_inc(aln_stats, 1)

            def norm_apply(q):
                dve.wait_ge(aln_rstd, q + 1)
                half = (q % 2) * (QB * GW)
                for t in range(QB * NT):
                    ins = dve.tensor_scalar(big[:, bass.ds(half + t * D, D)],
                                            xs[:, bass.ds(q * (QB * GW) + t * D, D)],
                                            mvA[:, t, 0:1], rsA[:, t:t + 1], ALU.subtract, ALU.mult)
                    if t < QB * NT - 1:
                        step.add(ins)
                ins.then_inc(aln_f, 1)

            def residual(q):
                half = (q % 2) * (QB * GW)
                for c in range(NT):
                    z = bank[4 + c % 2]
                    dve.wait_ge(a_z, q * NT + c + 1)
                    ta = ft[c % 2][:, :, :]
                    tb = ft[2 + c % 2][:, :, :]
                    step.add(dve.tensor_tensor(ta, z[:, :].rearrange("p (b d) -> p b d", b=QB), b2_bc[:, :, :], ALU.add))
                    step.wait()
                    dve.sem_inc(a_zfree, 1)
                    f = big[:, bass.ds(half, QB * GW)].rearrange("p (b c d) -> p b c d", b=QB, c=NT)[:, :, c, :]
                    dep(dve.scalar_tensor_tensor(out=tb, in0=ta, scalar=0.0, in1=f, op0=ALU.max, op1=ALU.add))
                    xv = xs[:, bass.ds(q * (QB * GW), QB * GW)].rearrange("p (b c d) -> p b c d", b=QB, c=NT)[:, :, c, :]
                    dep(dve.scalar_tensor_tensor(out=xv, in0=tb, scalar=0.5, in1=xv, op0=ALU.mult, op1=ALU.add))

            for q in range(4):
                dve.wait_ge(x_in[q], 16)
            norm_stats(0)
            norm_apply(0)
            AQ = B // QB
            step.clear()
            with dve.Fori(0, AQ - 1) as q:
                norm_stats(q + 1)
                norm_apply(q + 1)
                residual(q)
                step.clear()
            residual(AQ - 1)

            def stats(k, g, src=None):
                for c in range(NT):
                    step.add(dve.bn_stats(st[k][:, c, :], src[:, c, :] if src is not None
                                          else xs[:, bass.ds(g * GW + c * D, D)]))
                step.wait()
                for c in range(NT):
                    ins = dve.bn_aggr(mv[k][:, c, :], st[k][:, c, :])
                    if c < NT - 1:
                        step.add(ins)
                ins.then_inc(ln_stats[k], 1)

            def apply(k, n, g, src=None):
                dve.wait_ge(ln_rstd[k], n)
                for c in range(NT):
                    ins = dve.tensor_scalar(ft[k][:, c, :], src[:, c, :] if src is not None
                                            else xs[:, bass.ds(g * GW + c * D, D)],
                                            mv[k][:, c, 0:1], rs[k][:, c:c + 1], ALU.subtract, ALU.mult)
                    if c < NT - 1:
                        step.add(ins)
                ins.then_inc(ln_f[k], 1)

            def top2(k, E, bias):
                dep(dve.tensor_tensor(lg[k][:, :, 0:E], bank[2][:, 0:NT * E].rearrange("p (c e) -> p c e", c=NT),
                                      bias[:, :, :], ALU.add))
                for c in range(NT):
                    step.add(dve.max(mx[k][:, c, :], lg[k][:, c, :]))
                step.wait()
                for c in range(NT):
                    step.add(dve.max_index(ix[k][:, c, :], mx[k][:, c, :], lg[k][:, c, :]))
                step.wait()
                dep(dve.tensor_copy(ixf[k][:, :, :], ix[k][:, :, 0:2].rearrange("p c j -> p j c")))
                for j in range(2):
                    step.add(dve.tensor_tensor(oh[k][:, j, :, :], iota8[:, :, :],
                                               ixf[k][:, j, :].unsqueeze(2).broadcast_to([P, NT, 8]), ALU.is_equal))
                step.wait()

            def mix(k, dst, a, b):
                for j, w in ((0, a), (1, b)):
                    step.add(dve.tensor_tensor(oh[k][:, j, :, :], oh[k][:, j, :, :],
                                               w.unsqueeze(2).broadcast_to([P, NT, 8]), ALU.mult))
                step.wait()
                return dve.tensor_tensor(dst, oh[k][:, 0, :, :], oh[k][:, 1, :, :], ALU.add)

            def route_b1(n):
                dve.wait_ge(b_lp, n + 1)
                top2(0, EB, rb2_bc)
                step.add(dve.tensor_tensor(dl[0][:, :, :], lg[0][:, :, :],
                                           mx[0][:, :, 0:1].broadcast_to([P, NT, 8]), ALU.subtract))
                step.wait()
                dve.sem_inc(b_ask, 1)

            def route_b2(n):
                w = wt[0]
                dve.wait_ge(b_exp, n * 2 + 1)
                dep(dve.tensor_reduce(w[:, 0, :], ex[0][:, :, :], AX.X, ALU.add))
                dep(dve.reciprocal(w[:, 1, :], w[:, 0, :]))
                dep(dve.tensor_tensor(dl[0][:, :, :], ex[0][:, :, :], oh[0][:, 1, :, :], ALU.mult))
                dep(dve.tensor_reduce(w[:, 2, :], dl[0][:, :, :], AX.X, ALU.add))
                dep(dve.tensor_tensor(w[:, 2, :], w[:, 2, :], w[:, 1, :], ALU.mult))
                step.add(dve.tensor_tensor(w[:, 3, :], w[:, 2, :], w[:, 1, :], ALU.subtract))
                step.wait()
                dve.sem_inc(b_ask, 1)

            def route_b3(n):
                w = wt[0]
                dve.wait_ge(b_exp, n * 2 + 2)
                dep(dve.tensor_scalar(w[:, 5, :], w[:, 4, :], 1.0, None, ALU.add))
                dep(dve.reciprocal(w[:, 6, :], w[:, 5, :]))
                dep(dve.tensor_tensor(w[:, 7, :], w[:, 4, :], w[:, 6, :], ALU.mult))
                dep(mix(0, cB[:, :, :], w[:, 6, :], w[:, 7, :]))
                dve.sem_inc(b_c, 1)

            def combine(n, e):
                dve.wait_ge(b_op, n * EB + (e + 1))
                for c in range(NT):
                    xc = xs[:, bass.ds(n * GW + c * D, D)]
                    step.add(dve.scalar_tensor_tensor(out=xc, in0=bank[5 + e % 2][:, c * D:(c + 1) * D],
                                                      scalar=cB[:, c, e:e + 1], in1=xc, op0=ALU.mult, op1=ALU.add))
                step.wait()
                dve.sem_inc(b_ofree, 1)

            def body(n, cur, prev, nxt):
                if prev:
                    stats(1, n - 1)
                if cur:
                    route_b1(n)
                if prev:
                    apply(1, n, n - 1)
                if cur:
                    route_b2(n)
                    route_b3(n)
                    combine(n, 0)
                    combine(n, 1)
                if prev:
                    dve.wait_ge(c_p, n)
                    dve.wait_ge(c_b, n)
                    xg = grp(xs, n - 1)
                    dep(dve.tensor_tensor(xg, xg, bank[7][:, :], ALU.add))
                    stats(2, n - 1)
                if cur:
                    combine(n, 2)
                    dve.wait_ge(b_bias, n + 1)
                    xg = grp(xs, n)
                    dep(dve.tensor_tensor(xg, xg, bank[1][:, :], ALU.add))
                    dve.sem_inc(b_biasfree, 1)
                if prev:
                    apply(2, n, n - 1)
                    dve.wait_ge(ln_f[2], n)
                    stats(3, n - 1, ft[2])
                if cur:
                    combine(n, 3)
                if nxt:
                    stats(0, n + 1)
                if prev:
                    apply(3, n, n - 1, ft[2])
                    dve.wait_ge(d_lp, n)
                    top2(1, ED, br_bc)
                    w = wt[1]
                    dep(dve.tensor_tensor(w[:, 0, :], mx[1][:, :, 1], mx[1][:, :, 0], ALU.subtract))
                    dve.sem_inc(d_ask, 1)
                if cur:
                    combine(n, 4)
                if prev:
                    dve.wait_ge(d_exp, n)
                    dep(dve.tensor_scalar(w[:, 2, :], w[:, 1, :], 1.0, None, ALU.add))
                    dep(dve.reciprocal(w[:, 3, :], w[:, 2, :]))
                    dep(dve.tensor_tensor(w[:, 4, :], w[:, 1, :], w[:, 3, :], ALU.mult))
                    dep(mix(1, cD[:, bass.ds(n - 1, 1)].rearrange("p a c e -> p (a c) e"), w[:, 3, :], w[:, 4, :]))
                if nxt:
                    apply(0, n + 2, n + 1)
                if cur:
                    combine(n, 5)

            stats(0, 0)
            apply(0, 1, 0)
            pipeline(dve, body, step)

            step.clear()
            with dve.Fori(0, G) as g:
                dep(dve.tensor_copy(cDs[:, :, :], cD[:, bass.ds(g, 1)].rearrange("p a c e -> p (a c) e")))
                dve.sem_inc(e_cs, 1)
                dve.wait_ge(e_bias, g + 1)
                xg = grp(xs, g)
                dep(dve.tensor_tensor(xg, xg, bank[5][:, :], ALU.add))
                for e in range(ED):
                    dve.wait_ge(e_yp, g * ED + (e + 1))
                    for c in range(NT):
                        xc = xs[:, bass.ds(g * GW + c * D, D)]
                        step.add(dve.scalar_tensor_tensor(out=xc, in0=bank[2 + e % 2][:, c * D:(c + 1) * D],
                                                          scalar=cDs[:, c, e:e + 1], in1=xc,
                                                          op0=ALU.mult, op1=ALU.add))
                    step.wait()
                    dve.sem_inc(e_yfree, 1)
                dve.sem_inc(x_done, 1)
                step.clear()


_OUT = ((16, 512, 128), "float32")


def kernel(**inputs):
    import numpy as np
    import concourse.bacc as bacc
    from concourse import mybir as mb
    from concourse.bass_utils import run_bass_kernel_spmd as run

    a = {k: np.asarray(v) for k, v in inputs.items()}
    e_last = a["L1_ffn_W1"].shape[0]
    nodes = a["adj"].shape[0]
    tiles = nodes // 128

    def rows(v, n):
        return np.broadcast_to(v[None, None, :], (128, n, v.shape[0]))

    laid = {
        "x": a["x"], "adjT": a["adj"].T,
        "w1_loop": a["L0_gnn_w1_loop"], "w1_neigh": a["L0_gnn_w1_neigh"], "b1": a["L0_gnn_b1"][:, None],
        "w2_loop": a["L0_gnn_w2_loop"], "w2_neigh": a["L0_gnn_w2_neigh"], "b2": rows(a["L0_gnn_b2"], 4),
        "rw1": a["L0_ffn_router_w1"], "rb1": a["L0_ffn_router_b1"][:, None],
        "rw2": a["L0_ffn_router_w2"], "rb2": rows(a["L0_ffn_router_b2"], tiles),
        "ew1": a["L0_ffn_expert_w1"], "eb1": a["L0_ffn_expert_b1"].T,
        "ew2": a["L0_ffn_expert_w2"], "eb2": a["L0_ffn_expert_b2"].T,
        "ew3": a["L0_ffn_expert_w3"], "eb3": a["L0_ffn_expert_b3"],
        "nv1T": a["L1_gnn_node_vec1"].T, "nv2": a["L1_gnn_node_vec2"],
        "gW": a["L1_gnn_W"], "gb": rows(a["L1_gnn_b"], tiles),
        "Wr": a["L1_ffn_Wr"], "br": rows(a["L1_ffn_br"], tiles),
        "lngT": a["L1_ffn_ln_g"].T, "lnbT": a["L1_ffn_ln_b"].T,
        "W1": a["L1_ffn_W1"], "b1T": a["L1_ffn_b1"].reshape(e_last * 4, 128).T,
        "W2": a["L1_ffn_W2"], "b2e": a["L1_ffn_b2"],
    }
    nc = bacc.Bacc("TRN2", target_bir_lowering=False, num_devices=1)
    arrays, args = {}, []
    for name, v in laid.items():
        v = np.ascontiguousarray(v)
        arrays[f"in_{name}"] = v
        args.append(nc.dram_tensor(f"in_{name}", v.shape, mb.dt.from_np(v.dtype), kind="ExternalInput").ap())
    args.append(nc.dram_tensor("out_0", _OUT[0], mb.dt.from_np(np.dtype(_OUT[1])), kind="ExternalOutput").ap())
    program(nc, *args)
    r = run(nc, [arrays], core_ids=[0])
    return r.results[0]["out_0"]
```

```python
from contextlib import ExitStack

import concourse.bass as bass
from concourse import mybir

P = 128
F32 = mybir.dt.float32
U32 = mybir.dt.uint32
I32 = mybir.dt.int32
ALU = mybir.AluOpType
ACT = mybir.ActivationFunctionType
AX = mybir.AxisListType
LN_EPS = 1e-5
PAD_LOGIT = -1e30
SPLIT = 8
GAP = 2


class Steps:

    def __init__(self, eng, sem):
        self.eng, self.sem, self.n = eng, sem, 0

    def add(self, ins):
        ins.then_inc(self.sem, 1)
        self.n += 1

    def wait(self):
        self.eng.wait_ge(self.sem, self.n)

    def clear(self):
        if self.n:
            self.wait()
        self.eng.sem_clear(self.sem)
        self.n = 0


def program(nc, x, adjT, w1_loop, w1_neigh, b1, w2_loop, w2_neigh, b2, rw1, rb1, rw2, rb2, ew1, eb1, ew2, eb2,
            ew3, eb3, nv1T, nv2, gW, gb, Wr, br, lngT, lnbT, W1, b1T, W2, b2e, out):
    B, N, D = x.shape
    T = B * N
    NT = N // P
    G = T // N
    GW = NT * D
    EB = ew1.shape[0]
    RH = rw1.shape[1]
    ED = W1.shape[0]
    H = W1.shape[2]
    HC = H // P
    RANK = nv1T.shape[0]
    QB = 4
    PARTS = ((0, SPLIT), (SPLIT, G))
    BLK = 256
    BT = BLK // P
    NBS = [((g1 - g0) * N * 2 + ED * (BLK - 1)) // BLK for g0, g1 in PARTS]
    NB_ALL = sum(NBS)
    MT = max(g1 - g0 for g0, g1 in PARTS) * NT
    assert NB_ALL % 2 == 0
    FILLS = sum(-(-(nb * BLK) // T) for nb in NBS)
    Xd = [nc.dram_tensor(f"x_slots{k}", [nb * BLK, D], F32, kind="Internal").ap() for k, nb in enumerate(NBS)]
    Yd = [nc.dram_tensor(f"y_slots{k}", [nb * BLK, D], F32, kind="Internal").ap() for k, nb in enumerate(NBS)]

    ctx = ExitStack()
    with ctx:
        def sb(name, shape, dt=F32):
            return ctx.enter_context(nc.sbuf_tensor(name, shape, dt))

        def ps(name, shape):
            return ctx.enter_context(nc.psum_tensor(name, shape, F32))

        def carve(t, *shapes):
            at, pieces = 0, []
            for shape in shapes:
                size = 1
                for k in shape:
                    size *= k
                piece = t[:, at:at + size]
                if len(shape) == 2:
                    piece = piece.rearrange("p (a b) -> p a b", a=shape[0])
                elif len(shape) == 3:
                    piece = piece.rearrange("p (a b c) -> p a b c", a=shape[0], b=shape[1])
                pieces.append(piece)
                at += size
            return pieces

        def sem(name):
            return ctx.enter_context(nc.semaphore(name))

        xs = sb("xs", [P, G * GW])
        big = sb("big", [P, G * GW])
        fA = big[:, 0:2 * QB * GW].rearrange("p (h b n) -> p h b n", h=2, b=QB)
        adp = big[:, 8 * GW:8 * GW + NT * N].rearrange("p (c n) -> p c n", c=NT)
        dia = big[:, 12 * GW:12 * GW + NT * P].rearrange("p (c n) -> p c n", c=NT)
        adjT_sb = sb("adjT_sb", [P, NT, N])
        wA = sb("wA", [P, 4, D])
        b1_sb = sb("b1_sb", [P, 1])
        b2_bc = sb("b2_bc", [P, QB, D])
        rw1_sb = sb("rw1_sb", [P, RH])
        rb1_sb = sb("rb1_sb", [RH, 1])
        rw2_sb = sb("rw2_sb", [RH, EB])
        rb2_bc = sb("rb2_bc", [P, NT, EB])
        ew1_sb = sb("ew1_sb", [P, EB, D])
        ew2_sb = sb("ew2_sb", [P, EB, D])
        ew3_sb = sb("ew3_sb", [P, EB, D])
        eb1_sb = sb("eb1_sb", [P, EB])
        eb2_sb = sb("eb2_sb", [P, EB])
        eb3_sb = sb("eb3_sb", [EB, D])
        nv1T_sb = big[0:RANK, 14 * GW:14 * GW + N]
        nv2_sb = big[0:RANK, 15 * GW:15 * GW + N]
        gW_sb = sb("gW_sb", [P, 7, D])
        gb_bc = sb("gb_bc", [P, NT, D])
        Wr_sb = sb("Wr_sb", [P, ED])
        br_bc = sb("br_bc", [P, NT, ED])
        lngT_sb = sb("lngT_sb", [P, ED])
        lnbT_sb = sb("lnbT_sb", [P, ED])
        W1b = sb("W1b", [P, ED, H + HC])
        W2b = sb("W2b", [P, ED, H + D])
        W1_sb = W1b[:, :, 0:H]
        b1_of = W1b[:, :, H:H + HC]
        ident = sb("ident", [P, P])
        ones = sb("ones", [P, P])
        iota8 = sb("iota8", [P, NT, 8])
        eps = sb("eps", [P, QB * NT])
        neg_half = sb("neg_half", [P, QB * NT])
        s1_bc = sb("s1_bc", [P, N])
        s2_bc = sb("s2_bc", [P, N])
        a1_bc = sb("a1_bc", [P, N])
        a2_bc = sb("a2_bc", [P, N])
        adm = sb("adm", [P, 4, NT])
        st = [sb(f"st{k}", [P, NT, 6]) for k in range(4)]
        mv = [sb(f"mv{k}", [P, NT, 2]) for k in range(4)]
        ve = [sb(f"ve{k}", [P, NT]) for k in range(4)]
        rs = [sb(f"rs{k}", [P, NT]) for k in range(4)]
        ft = [sb(f"ft{k}", [P, NT, D]) for k in range(4)]
        fT = [sb(f"fT{k}", [P, 2 * N if k == 0 else N]) for k in range(3)]
        stA = sb("stA", [P, QB * NT, 6])
        mvA = sb("mvA", [P, QB * NT, 2])
        veA = sb("veA", [P, QB * NT])
        rsA = sb("rsA", [P, QB * NT])
        work = sb("work", [P, 4 * N])
        uT, fTA = carve(work, (2, N), (2, N))
        xst, seen, tot, cum = carve(work, (2, NT, D), (ED * MT,), (ED * MT,), (ED * MT,))
        hT = sb("hT", [P, 2, HC, N])
        h1A = hT[:, 0]
        gA = hT[:, 1].rearrange("p m (b d) -> p m b d", b=QB)
        rhT = sb("rhT", [RH, N])
        h1T, h2T, fs = carve(hT[:, :, :, :].rearrange("p a b n -> p (a b n)"), (2, N), (2, N), (4, N))
        lg = [sb(f"lg{k}", [P, NT, 8]) for k in range(2)]
        mx = [sb(f"mx{k}", [P, NT, 8]) for k in range(2)]
        ix = [sb(f"ix{k}", [P, NT, 8], U32) for k in range(2)]
        ixf = [sb(f"ixf{k}", [P, 2, NT]) for k in range(2)]
        oh = [sb(f"oh{k}", [P, 2, NT, 8]) for k in range(2)]
        dl = [sb(f"dl{k}", [P, NT, 8]) for k in range(2)]
        ex = [sb(f"ex{k}", [P, NT, 8]) for k in range(2)]
        wt = [sb(f"wt{k}", [P, 8, NT]) for k in range(2)]
        cB = sb("cB", [P, NT, 8])
        ohD = sb("ohD", [P, 2, ED, G * NT])
        wD = sb("wD", [P, 2, G * NT])
        slot = sb("slot", [P, 2, G * NT], U32)
        tri = sb("tri", [P, P])
        onesr = sb("onesr", [P, ED * MT])
        cnt = sb("cnt", [P, 6, ED])
        cnti = sb("cnti", [P, 2, ED], I32)
        iotab = sb("iotab", [1, NB_ALL])
        blkc = sb("blkc", [1, NB_ALL, ED - 1])
        blkf = sb("blkf", [1, NB_ALL])
        blk_e = sb("blk_e", [1, NB_ALL], I32)
        wc = sb("wc", [P, 2, NT])
        ist = sb("ist", [P, 2, 2, NT], U32)
        igt = sb("igt", [P, 2, 2, NT], U32)
        W1s, W2s, xb, xT, yb = carve(big[:, 0:SPLIT * GW], (2, H + HC), (2, H + D), (2, BT, D), (2, BLK), (2, BT, D))
        yg = carve(big[:, SPLIT * GW:], (2, NT, D), (2, NT, D))
        cT = sb("cT", [8, N])

        bank = [ps(f"bank{k}", [P, 512]) for k in range(8)]

        x_in = [sem(f"x_in{q}") for q in range(4)]
        nv_in, w_first, w_in = sem("nv_in"), sem("w_first"), sem("w_in")
        x_out = sem("x_out")
        pool_step = sem("pool_step")
        dve_step = sem("dve_step")
        act_step = sem("act_step")
        consts = sem("consts")
        scores_p, scores_relu, scores_max, scores_exp, scores_dia = [
            sem("scores_" + s) for s in "p relu max exp dia".split()]
        adj_sums_p, soft_sums_p, offset_p, factors, gains = [
            sem(s) for s in "adj_sums_p soft_sums_p offset_p factors gains".split()]
        ln_stats = [sem(f"ln_stats{k}") for k in range(4)]
        ln_rstd = [sem(f"ln_rstd{k}") for k in range(4)]
        ln_f = [sem(f"ln_f{k}") for k in range(4)]
        turned = [sem(f"turned{k}") for k in range(4)]
        turned_sb = [sem(f"turned_sb{k}") for k in range(4)]
        aln_stats, aln_rstd, aln_f = sem("aln_stats"), sem("aln_rstd"), sem("aln_f")
        a_fp, a_fT, a_up, a_uT, a_hp, a_h, a_gp, a_g, a_z, a_zfree = [
            sem("a_" + s) for s in "fp fT up uT hp h gp g z zfree".split()]
        b_rp, b_rh, b_lp, b_lfree, b_hp, b_h, b_op, b_ofree, b_c, b_cp, b_cT, b_bias, b_biasfree, b_ask, b_exp = [
            sem("b_" + s) for s in "rp rh lp lfree hp h op ofree c cp cT bias biasfree ask exp".split()]
        c_fs, c_p, c_b = [sem("c_" + s) for s in "fs p b".split()]
        d_lp, d_ask, d_exp = [sem("d_" + s) for s in "lp ask exp".split()]
        x_done = sem("x_done")
        slots_set = sem("slots_set")
        seen_ready, ranks_p, routed = sem("seen_ready"), sem("ranks_p"), sem("routed")
        staged, scattered = sem("staged"), [sem(f"scattered{k}") for k in range(2)]
        xb_in = [sem(f"xb_in{k}") for k in range(2)]
        y_out = [sem(f"y_out{k}") for k in range(2)]
        gathered = [sem(f"gathered{k}") for k in range(2)]
        g_used = sem("g_used")
        e_tp, e_xT, e_w1, e_w2, e_hp, e_h, e_yp, e_y = [
            sem("e_" + s) for s in "tp xT w1 w2 hp h yp y".split()]

        xr = x.rearrange("b (c p) d -> p b c d", p=P)
        xs_v = xs[:, :].rearrange("p (b c d) -> p b c d", b=B, c=NT)

        first_loads = [
            (adjT_sb[:, :, :], adjT.rearrange("(c p) n -> p c n", p=P)),
            (wA[:, 0, :], w1_loop), (wA[:, 1, :], w1_neigh), (wA[:, 2, :], w2_loop), (wA[:, 3, :], w2_neigh),
            (b1_sb[:, :], b1), (b2_bc[:, :, :], b2),
        ]
        loads = [
            (rw1_sb[:, :], rw1), (rb1_sb[:, :], rb1), (rw2_sb[:, :], rw2),
            (rb2_bc[:, :, :], rb2),
            (ew1_sb[:, :, :], ew1.rearrange("e d h -> d e h")),
            (ew2_sb[:, :, :], ew2.rearrange("e d h -> d e h")),
            (ew3_sb[:, :, :], ew3.rearrange("e d h -> d e h")),
            (eb1_sb[:, :], eb1), (eb2_sb[:, :], eb2), (eb3_sb[:, :], eb3),
            (gW_sb[:, :, :], gW.rearrange("(k p) n -> p k n", p=P)),
            (gb_bc[:, :, :], gb),
            (Wr_sb[:, :], Wr), (br_bc[:, :, :], br),
            (lngT_sb[:, :], lngT), (lnbT_sb[:, :], lnbT),
            (W1_sb, W1.rearrange("e d h -> d e h")),
            (b1_of, b1T),
            (W2b[:, :, 0:H], W2),
            (W2b[:, :, H:H + D], b2e),
        ]
        W_FIRST = 16 * len(first_loads)
        W_IN = 16 * len(loads)

        HID = [(1, 0), (1, 1), (2, 0), (1, 2), (2, 1), (1, 3), (2, 2), (1, 4), (2, 3), (1, 5), (2, 4), (2, 5)]
        NH = len(HID)

        assert G == 2 * SPLIT and SPLIT % 2 == 0
        PER_SCATTER = 16 * 2 * NT
        SCATTERED = [[PER_SCATTER * SPLIT, 0], [PER_SCATTER * (SPLIT + SPLIT // 2), PER_SCATTER * (SPLIT // 2)]]

        block = ctx.enter_context(nc.Block())

        def fT0(m):
            return fT[0][:, bass.ds((m % 2) * N, N)]

        def grp(t, g, w=GW):
            return t[:, bass.ds(g * w, w)]

        def pipeline(eng, body, steps=None, at_route=None, after=None):
            def loop(a, b, part):
                if a < b:
                    if steps:
                        steps.clear()
                    with eng.Fori(a, b) as n:
                        body(n, True, True, True, part)
                        if steps:
                            steps.clear()

            body(-1, False, False, True, 0)
            if after:
                after(-1)
            body(0, True, False, True, 0)
            if after:
                after(0)
            loop(1, SPLIT + 1, 0)
            if at_route:
                at_route(0)
            body(SPLIT + 1, True, True, True, 1)
            loop(SPLIT + 2, G - 1, 1)
            body(G - 1, True, True, False, 1)
            body(G, False, True, False, 1)
            if at_route:
                at_route(1)

        @block.sync
        def _(sp):
            sp.dma_start(nv1T_sb, nv1T).then_inc(nv_in, 16)
            sp.dma_start(nv2_sb, nv2).then_inc(nv_in, 16)

            def load_x(q):
                sp.dma_start(xs_v[:, QB * q:QB * q + QB], xr[:, QB * q:QB * q + QB]).then_inc(x_in[q], 16)

            load_x(0)
            for dst, src in first_loads:
                sp.dma_start(dst, src).then_inc(w_first, 16)
            for q in range(1, 4):
                load_x(q)
            for dst, src in loads:
                sp.dma_start(dst, src).then_inc(w_in, 16)
            x_rows = x.rearrange("b n d -> (b n) d").rearrange("(p r) d -> p (r d)", p=P)
            for part, nb in enumerate(NBS):
                rows = nb * BLK // P
                Xi = Xd[part].rearrange("(p r) d -> p (r d)", p=P)
                for r in range(0, rows, G * NT):
                    k = min(G * NT, rows - r)
                    sp.dma_start(Xi[:, r * D:(r + k) * D], x_rows[:, 0:k * D]).then_inc(slots_set, 16)

            def rows_of(slots, j, part):
                return slots[part][bass.ds((j - sum(NBS[:part])) * BLK, BLK), :].rearrange("(t p) d -> p t d", p=P)

            def load(j, par, part):
                if not (isinstance(j, int) and j < 2):
                    sp.wait_ge(e_tp, j - 1)
                sp.dma_start(xb[:, par, :, :], rows_of(Xd, j, part)).then_inc(xb_in[par], 16)

            def store(j, par, part):
                sp.wait_ge(e_y, j + 1)
                sp.dma_start(rows_of(Yd, j, part), yb[:, par, :, :]).then_inc(y_out[par], 16)

            def part_in(part):
                for k in range(2):
                    if SCATTERED[part][k]:
                        sp.wait_ge(scattered[k], SCATTERED[part][k])

            cut = NBS[0]
            part_in(0)
            for j in range(4):
                load(j, j % 2, 0)

            def step(t):
                if t + 3 == cut:
                    part_in(1)
                if t + 3 < NB_ALL:
                    load(t + 3, (t + 3) % 2, int(t + 3 >= cut))
                store(t - 1, (t - 1) % 2, int(t - 1 >= cut))

            def steps(t0, t1, part):
                with sp.Fori(0, (t1 - t0) // 2) as i:
                    for k in range(2):
                        load(i * 2 + (t0 + k + 3), k, part)
                        store(i * 2 + (t0 + k - 1), k, part)
                return t0 + (t1 - t0) // 2 * 2

            assert cut > 4
            for t in range(steps(1, cut - 3, 0), cut + 1):
                step(t)
            t = cut + 1
            if t % 2 == 0:
                step(t)
                t += 1
            for t in range(steps(t, NB_ALL - 3, 1), NB_ALL + 1):
                step(t)
            with sp.Fori(0, G) as g:
                sp.wait_ge(x_done, g + 1)
                sp.dma_start(out[bass.ds(g, 1)].rearrange("b (c p) d -> p (b c) d", p=P),
                             grp(xs, g).rearrange("p (c d) -> p c d", c=NT)).then_inc(x_out, 16)
            sp.wait_ge(x_out, 16 * G)

        @block.gpsimd
        def _(pool):
            step = Steps(pool, pool_step)
            step.add(pool.memset(ident[:, :], 0.0))
            pool.memset(ones[:, :], 1.0).then_inc(consts, 1)
            pool.memset(neg_half[:, :], -0.5).then_inc(consts, 1)
            pool.memset(eps[:, :], LN_EPS).then_inc(consts, 1)
            for k in range(2):
                pool.memset(lg[k][:, :, :], PAD_LOGIT).then_inc(consts, 1)
            pool.memset(onesr[:, :], 1.0).then_inc(consts, 1)
            step.add(pool.memset(tri[:, :], 0.0))
            pool.iota(iotab[:, :], [[1, NB_ALL]], channel_multiplier=0,
                      allow_small_or_imprecise_dtypes=True).then_inc(consts, 1)
            pool.iota(iota8[:, :, :], [[0, NT], [1, 8]], channel_multiplier=0,
                      allow_small_or_imprecise_dtypes=True).then_inc(consts, 1)
            step.wait()
            pool.affine_select(out=ident[:, :], in_=ident[:, :], compare_op=ALU.not_equal, fill=1.0, base=0,
                               pattern=[[-1, P]], channel_multiplier=1).then_inc(consts, 1)
            pool.affine_select(out=tri[:, :], in_=tri[:, :], compare_op=ALU.is_ge, fill=1.0, base=0,
                               pattern=[[-1, P]], channel_multiplier=1).then_inc(consts, 1)
            pool.wait_ge(consts, 10)

            step.clear()
            with pool.Fori(0, B // QB) as q:
                pool.wait_ge(aln_stats, q + 1)
                step.add(pool.tensor_tensor(veA[:, :], mvA[:, :, 1], eps[:, :], ALU.add))
                step.wait()
                pool.tensor_tensor(rsA[:, :], veA[:, :], neg_half[:, :], ALU.pow).then_inc(aln_rstd, 1)
                step.clear()

            def rstd(k, n):
                pool.wait_ge(ln_stats[k], n)
                step.add(pool.tensor_tensor(ve[k][:, :], mv[k][:, :, 1], eps[:, 0:NT], ALU.add))
                step.wait()
                pool.tensor_tensor(rs[k][:, :], ve[k][:, :], neg_half[:, 0:NT], ALU.pow).then_inc(ln_rstd[k], 1)

            def stage(m, k, turn):
                if not (isinstance(turn, int) and turn == 0):
                    pool.wait_ge(scattered[k], turn * PER_SCATTER)
                pool.tensor_copy(xst[:, k, :, :].rearrange("p c d -> p (c d)"), grp(big, m)).then_inc(staged, 1)
                pool.wait_ge(staged, m + 1)
                step.add(pool.tensor_copy(ist[:, k, :, :], slot[:, :, bass.ds(m * NT, NT)]))
                step.wait()

            def send(k, part, tiles):
                for c in tiles:
                    for j in range(2):
                        pool.indirect_dma_start(Xd[part][:, :],
                                                bass.IndirectOffsetOnAxis(ap=ist[:, k, j, c:c + 1], axis=0),
                                                xst[:, k, c, :], None).then_inc(scattered[k], 16)

            def body(n, cur, prev, nxt, part):
                if prev:
                    rstd(1, n)
                if nxt:
                    rstd(0, n + 2)
                if prev:
                    pool.wait_ge(turned_sb[1], n)
                    for k, by in enumerate((s1_bc, s2_bc, a1_bc, a2_bc)):
                        pool.tensor_tensor(fs[:, k, :], fT[1][:, :], by[:, :], ALU.mult).then_inc(c_fs, 1)
                    pool.wait_ge(ln_f[1], n)
                    pool.tensor_tensor(grp(xs, n - 1), grp(xs, n - 1), gb_bc[:, :, :].rearrange("p a b -> p (a b)"),
                                       ALU.add).then_inc(c_b, 1)
                if part == 1:
                    m = n - (SPLIT + 1)
                    stage(m, 0, m)
                    send(0, 0, range(0, NT // 2))
                if prev:
                    rstd(2, n)
                    rstd(3, n)
                if part == 1:
                    send(0, 0, range(NT // 2, NT))

            def at_route(part):
                if part == 0:
                    pool.wait_ge(offset_p, 1)
                    for e in range(ED):
                        pool.tensor_tensor(W1b[:, e, 0:H], W1b[:, e, 0:H], lngT_sb[:, e:e + 1].broadcast_to([P, H]),
                                           ALU.mult).then_inc(gains, 1)
                    pool.wait_ge(slots_set, 16 * FILLS)
                pool.wait_ge(routed, part + 1)

            def after(n):
                if n == 0:
                    pool.wait_ge(factors, 1)

            pool.wait_ge(w_in, W_IN)
            pipeline(pool, body, step, at_route, after)
            for k in range(2):
                stage(SPLIT + k, k, SPLIT if k == 0 else 0)
                send(k, 1, range(NT))
            step.clear()
            with pool.Fori(1, (G - SPLIT) // 2) as i:
                for k in range(2):
                    stage(i * 2 + (SPLIT + k), k, i + (SPLIT if k == 0 else 0))
                    send(k, 1, range(NT))
                step.clear()

            def gather(m, k, turn, part):
                if not (isinstance(turn, int) and turn == 0):
                    pool.wait_ge(g_used, m - 1)
                step.add(pool.tensor_copy(igt[:, k, :, :], slot[:, :, bass.ds(m * NT, NT)]))
                step.wait()
                for c in range(NT):
                    for j in range(2):
                        pool.indirect_dma_start(yg[k][:, j, c, :], None, Yd[part][:, :],
                                                bass.IndirectOffsetOnAxis(ap=igt[:, k, j, c:c + 1], axis=0)
                                                ).then_inc(gathered[k], 16)

            for part, (g0, g1) in enumerate(PARTS):
                done = sum(NBS[:part + 1])
                pool.wait_ge(y_out[0], 16 * ((done + 1) // 2))
                pool.wait_ge(y_out[1], 16 * (done // 2))
                if part == 0:
                    gather(0, 0, 0, part)
                    gather(1, 1, 0, part)
                a = 1 if part == 0 else g0 // 2
                step.clear()
                with pool.Fori(a, g1 // 2) as i:
                    for k in range(2):
                        gather(i * 2 + k, k, 1, part)
                    step.clear()

        @block.tensor
        def _(pe):
            mm = pe.matmul
            pe.wait_ge(consts, 10)
            pe.wait_ge(nv_in, 32)
            for c in range(NT):
                mm(bank[4 + c][:, :], nv1T_sb[:, c * P:(c + 1) * P], nv2_sb, start=True, stop=True).then_inc(scores_p, 1)
            pe.wait_ge(w_first, W_FIRST)
            pe.wait_ge(scores_relu, NT)
            for m in range(NT):
                ins = mm(bank[6][:, :], ones[:, :], adjT_sb[:, m, :], start=(m == 0), stop=(m == NT - 1))
            ins.then_inc(adj_sums_p, 1)

            def first_layer(q, half, i):
                f = fA[:, half]
                done = q * QB

                def turn(b):
                    if b == 0:
                        pe.wait_ge(aln_f, q + 1)
                    if b > 0:
                        pe.wait_ge(a_fT, done + b)
                    for c in range(NT):
                        ins = pe.transpose(bank[0][:, c * P:(c + 1) * P], f[:, b, c * D:(c + 1) * D], ident[:, :])
                    ins.then_inc(a_fp, 1)

                def neigh(b):
                    if b > 0:
                        pe.wait_ge(a_uT, done + b)
                    for m in range(NT):
                        ins = mm(bank[1][:, :], f[:, b, m * D:(m + 1) * D], adjT_sb[:, m, :],
                                 start=(m == 0), stop=(m == NT - 1))
                    ins.then_inc(a_up, 1)

                def hidden(b):
                    pe.wait_ge(a_fT, done + b + 1)
                    pe.wait_ge(a_uT, done + b + 1)
                    if b > 0:
                        pe.wait_ge(a_h, done + b)
                    mm(bank[2][:, :], wA[:, 0, :], fTA[:, b % 2, :], start=True, stop=False)
                    mm(bank[2][:, :], wA[:, 1, :], uT[:, b % 2, :], start=False, stop=True).then_inc(a_hp, 1)

                def second(b):
                    pe.wait_ge(a_h, done + b + 1)
                    if b > 0:
                        pe.wait_ge(a_g, done + b)
                    for m in range(NT):
                        ins = mm(bank[3][:, m * D:(m + 1) * D], h1A[:, b, m * P:(m + 1) * P], wA[:, 3, :],
                                 start=True, stop=True)
                    ins.then_inc(a_gp, 1)

                turn(0)
                neigh(0)
                turn(1)
                hidden(0)
                neigh(1)
                turn(2)
                hidden(1)
                second(0)
                neigh(2)
                turn(3)
                hidden(2)
                second(1)
                neigh(3)
                second(2)
                hidden(3)
                second(3)
                pe.wait_ge(a_g, done + QB)
                for c in range(NT):
                    pe.wait_ge(a_zfree, q * NT + (c + 1))
                    z = bank[4 + c % 2]
                    for m in range(NT):
                        mm(z[:, :], adjT_sb[:, m, c * P:(c + 1) * P], gA[:, m, :, :], start=(m == 0), stop=(m == NT - 1))
                    for b in range(QB):
                        ins = mm(z[:, b * D:(b + 1) * D], h1A[:, b, c * P:(c + 1) * P], wA[:, 2, :],
                                 start=False, stop=True, skip_group_check=True)
                    ins.then_inc(a_z, 1)

            with pe.Fori(0, B // QB // 2) as i:
                for half in range(2):
                    first_layer(i * 2 + half, half, i)

            def turn(k, n, bank_free=None):
                if bank_free:
                    pe.wait_ge(*bank_free)
                pe.wait_ge(ln_f[k], n)
                for c in range(NT):
                    ins = pe.transpose(bank[0][:, c * P:(c + 1) * P], ft[k][:, c, :], ident[:, :])
                ins.then_inc(turned[k], 1)

            def hid(n, j):
                layer, e = HID[j]
                if layer == 2:
                    pe.wait_ge(b_h, n * NH + (HID.index((1, e)) + 1))
                if not (isinstance(n, int) and n == 0 and j < 2):
                    pe.wait_ge(b_h, n * NH + (j - 1))
                w, f = (ew1_sb, fT0(n)) if layer == 1 else (ew2_sb, h1T[:, e % 2, :])
                mm(bank[3 + j % 2][:, :], w[:, e, :], f, start=True, stop=True).then_inc(b_hp, 1)

            def outp(n, e):
                pe.wait_ge(b_h, n * NH + (HID.index((2, e)) + 1))
                if not (isinstance(n, int) and n == 0 and e < 2):
                    pe.wait_ge(b_ofree, n * EB + (e - 1))
                for c in range(NT):
                    ins = mm(bank[5 + e % 2][:, c * D:(c + 1) * D], h2T[:, e % 2, c * P:(c + 1) * P], ew3_sb[:, e, :],
                             start=True, stop=True)
                ins.then_inc(b_op, 1)

            def body(n, cur, prev, nxt, part):
                if cur:
                    hid(n, 0)
                    hid(n, 1)
                    pe.wait_ge(b_c, n + 1)
                    for c in range(NT):
                        ins = pe.transpose(bank[1][0:8, c * P:(c + 1) * P], cB[:, c, :], ident[:, :])
                    ins.then_inc(b_cp, 1)
                    hid(n, 2)
                    hid(n, 3)
                    hid(n, 4)
                    outp(n, 0)
                    pe.wait_ge(b_cT, n + 1)
                    for c in range(NT):
                        ins = mm(bank[1][:, c * D:(c + 1) * D], cT[0:EB, c * P:(c + 1) * P], eb3_sb[:, :],
                                 start=True, stop=True)
                    ins.then_inc(b_bias, 1)
                if prev:
                    turn(1, n)
                if cur:
                    hid(n, 5)
                    hid(n, 6)
                    outp(n, 1)
                if nxt:
                    turn(0, n + 2, (turned_sb[1], n) if prev else None)
                if cur:
                    hid(n, 7)
                    hid(n, 8)
                    outp(n, 2)
                if nxt:
                    pe.wait_ge(turned_sb[0], n + 2)
                    if cur:
                        pe.wait_ge(b_biasfree, n + 1)
                    mm(bank[1][0:RH, :], rw1_sb[:, :], fT0(n + 1), start=True, stop=True).then_inc(b_rp, 1)
                if prev:
                    pe.wait_ge(c_fs, n * 4)
                    if part == 1:
                        pe.wait_ge(routed, 1)
                    for c in range(NT):
                        for k in range(5):
                            f = fT[1][:, c * P:(c + 1) * P] if k == 0 else fs[:, k - 1, c * P:(c + 1) * P]
                            w = gW_sb[:, k if k < 3 else k + 2, :]
                            ins = mm(bank[7][:, c * D:(c + 1) * D], f, w, start=(k == 0), stop=(k == 4))
                    ins.then_inc(c_p, 1)
                if nxt:
                    pe.wait_ge(b_rh, n + 2)
                    for c in range(NT):
                        ins = mm(bank[2][:, c * EB:(c + 1) * EB], rhT[:, c * P:(c + 1) * P], rw2_sb[:, :],
                                 start=True, stop=True)
                    ins.then_inc(b_lp, 1)
                if cur:
                    hid(n, 9)
                    hid(n, 10)
                    outp(n, 3)
                    hid(n, 11)
                if prev:
                    turn(2, n, (turned_sb[0], n + 2) if nxt else (turned_sb[1], n))
                if cur:
                    outp(n, 4)
                if prev:
                    pe.wait_ge(turned_sb[2], n)
                    for c in range(NT):
                        ins = mm(bank[2][:, c * ED:(c + 1) * ED], fT[2][:, c * P:(c + 1) * P], Wr_sb[:, :],
                                 start=True, stop=True)
                    ins.then_inc(d_lp, 1)
                if cur:
                    outp(n, 5)

            def at_route(part):
                g0, g1 = PARTS[part]
                w = ED * NT * (g1 - g0)
                pe.wait_ge(seen_ready, part + 1)
                mm(bank[7][:, 0:w], tri[:, :], seen[:, 0:w], start=True, stop=True)
                mm(bank[7][:, w:2 * w], ones[:, :], seen[:, 0:w], start=True, stop=True,
                   skip_group_check=True).then_inc(ranks_p, 1)

            pe.wait_ge(scores_dia, 1)
            for c in range(NT):
                ins = mm(bank[7][:, c * P:(c + 1) * P], ones[:, :], dia[:, c, :], start=True, stop=True)
            ins.then_inc(soft_sums_p, 1)
            pe.wait_ge(a_zfree, G + 2)
            pe.wait_ge(w_in, W_IN)
            for e in range(ED):
                for c in range(HC):
                    k = e * HC + c
                    ins = mm(bank[5][:, k:k + 1], W1b[:, e, c * P:(c + 1) * P], lnbT_sb[:, e:e + 1],
                             start=True, stop=True)
            ins.then_inc(offset_p, 1)
            pipeline(pe, body, None, at_route)

            def turn_block(j, par):
                pe.wait_ge(xb_in[par], (j // 2) * 16 + 16)
                if not (isinstance(j, int) and j < 1):
                    pe.wait_ge(e_xT, j)
                for t in range(BT):
                    ins = pe.transpose(bank[0][:, t * P:(t + 1) * P], xb[:, par, t, :], ident[:, :])
                ins.then_inc(e_tp, 1)

            def hidden(j, par):
                pe.wait_ge(e_xT, j + 1)
                pe.wait_ge(e_w1, j + 1)
                if not (isinstance(j, int) and j < 2):
                    pe.wait_ge(e_h, j * HC - HC)
                for c in range(HC):
                    z = bank[1 + 2 * par + c // 2]
                    ins = mm(z[:, (c % 2) * BLK:(c % 2 + 1) * BLK], W1s[:, par, c * P:(c + 1) * P], xT[:, par, :],
                             start=True, stop=True)
                    if c % 2:
                        ins.then_inc(e_hp, 1)

            def outer(j, par):
                pe.wait_ge(e_h, j * HC + HC)
                pe.wait_ge(e_w2, j + 1)
                if not (isinstance(j, int) and j < 2):
                    pe.wait_ge(e_y, j - 1)
                for t in range(BT):
                    for k in range(HC):
                        ins = mm(bank[5 + par][:, t * D:(t + 1) * D], hT[:, par, k, t * P:(t + 1) * P],
                                 W2s[:, par, k * D:(k + 1) * D], start=(k == 0), stop=(k == HC - 1))
                ins.then_inc(e_yp, 1)

            turn_block(0, 0)
            hidden(0, 0)
            turn_block(1, 1)
            hidden(1, 1)
            turn_block(2, 0)
            outer(0, 0)
            with pe.Fori(1, NB_ALL // 2 - 1) as i:
                for par in range(2):
                    hidden(i * 2 + par, par)
                    turn_block(i * 2 + (par + 1), 1 - par)
                    outer(i * 2 + (par - 1), 1 - par)
            j = NB_ALL - 2
            hidden(j, 0)
            turn_block(j + 1, 1)
            outer(j - 1, 1)
            hidden(j + 1, 1)
            outer(j, 0)
            outer(j + 1, 1)

        @block.scalar
        def _(act):
            step = Steps(act, act_step)
            for c in range(NT):
                act.wait_ge(scores_p, c + 1)
                act.activation(adp[:, c, :], bank[4 + c][:, :], ACT.Relu).then_inc(scores_relu, 1)
            for c in range(NT):
                act.wait_ge(scores_max, c + 1)
                act.activation(adp[:, c, :], adp[:, c, :], ACT.Exp, bias=adm[:, 0, c:c + 1]).then_inc(scores_exp, 1)
            act.wait_ge(w_first, W_FIRST)

            def first_layer(q):
                done = q * QB

                def copies(b):
                    act.wait_ge(a_fp, done + b + 1)
                    if b >= 2:
                        act.wait_ge(a_hp, done + b - 1)
                    act.copy(fTA[:, b % 2, :], bank[0][:, :]).then_inc(a_fT, 1)

                def copies2(b):
                    act.wait_ge(a_up, done + b + 1)
                    act.copy(uT[:, b % 2, :], bank[1][:, :]).then_inc(a_uT, 1)

                def relu(b):
                    act.wait_ge(a_hp, done + b + 1)
                    act.activation(h1A[:, b, :], bank[2][:, :], ACT.Relu, bias=b1_sb[:, :]).then_inc(a_h, 1)

                def second(b):
                    act.wait_ge(a_gp, done + b + 1)
                    act.copy(gA[:, :, b, :], bank[3][:, :].rearrange("p (m d) -> p m d", m=NT)).then_inc(a_g, 1)

                copies(0)
                copies2(0)
                copies(1)
                relu(0)
                copies2(1)
                copies(2)
                relu(1)
                second(0)
                copies2(2)
                copies(3)
                relu(2)
                second(1)
                copies2(3)
                second(2)
                relu(3)
                second(3)

            with act.Fori(0, B // QB) as q:
                first_layer(q)

            def turned_copy(k, n, dst):
                act.wait_ge(turned[k], n)
                act.copy(dst, bank[0][:, :]).then_inc(turned_sb[k], 1)

            def hid(n, j):
                layer, e = HID[j]
                act.wait_ge(b_hp, n * NH + (j + 1))
                if e >= 2 and layer == 1:
                    act.wait_ge(b_hp, n * NH + (HID.index((2, e - 2)) + 1))
                if e >= 2 and layer == 2:
                    act.wait_ge(b_op, n * EB + (e - 1))
                dst, b = (h1T, eb1_sb) if layer == 1 else (h2T, eb2_sb)
                act.activation(dst[:, e % 2, :], bank[3 + j % 2][:, :], ACT.Relu, bias=b[:, e:e + 1]).then_inc(b_h, 1)

            def body(n, cur, prev, nxt, part):
                if cur:
                    hid(n, 0)
                    hid(n, 1)
                    act.wait_ge(b_cp, n + 1)
                    act.copy(cT[:, :], bank[1][0:8, :]).then_inc(b_cT, 1)
                    hid(n, 2)
                    hid(n, 3)
                    hid(n, 4)
                if prev:
                    turned_copy(1, n, fT[1][:, :])
                if cur:
                    hid(n, 5)
                    hid(n, 6)
                if nxt:
                    turned_copy(0, n + 2, fT0(n + 1))
                if cur:
                    hid(n, 7)
                    hid(n, 8)
                if nxt:
                    act.wait_ge(b_rp, n + 2)
                    act.activation(rhT[:, :], bank[1][0:RH, :], ACT.Relu, bias=rb1_sb[:, :]).then_inc(b_rh, 1)
                if cur:
                    hid(n, 9)
                if nxt:
                    act.wait_ge(b_ask, n * 2 + 3)
                    act.activation(ex[0][:, :, :], dl[0][:, :, :], ACT.Exp).then_inc(b_exp, 1)
                if cur:
                    hid(n, 10)
                    hid(n, 11)
                if nxt:
                    act.wait_ge(b_ask, n * 2 + 4)
                    act.activation(wt[0][:, 4, :], wt[0][:, 3, :], ACT.Exp).then_inc(b_exp, 1)
                if prev:
                    turned_copy(2, n, fT[2][:, :])
                    act.wait_ge(d_ask, n)
                    act.activation(wt[1][:, 1, :], wt[1][:, 0, :], ACT.Exp).then_inc(d_exp, 1)

            act.wait_ge(w_in, W_IN)
            pipeline(act, body)

            def gelus(j, par):
                for c in range(HC):
                    if c % 2 == 0:
                        act.wait_ge(e_hp, j * 2 + (c // 2 + 1))
                    if c == 0 and not (isinstance(j, int) and j < 2):
                        act.wait_ge(e_yp, j - 1)
                    act.activation(hT[:, par, c, 0:BLK], bank[1 + 2 * par + c // 2][:, (c % 2) * BLK:(c % 2 + 1) * BLK],
                                   ACT.Gelu, bias=W1s[:, par, H + c:H + c + 1]).then_inc(e_h, 1)

            gelus(0, 0)
            gelus(1, 1)
            with act.Fori(1, NB_ALL // 2) as i:
                for par in range(2):
                    gelus(i * 2 + par, par)

        @block.vector
        def _(dve):
            step = Steps(dve, dve_step)

            def dep(ins):
                step.add(ins)
                step.wait()

            dve.sem_inc(a_zfree, 2)
            dve.wait_ge(consts, 10)
            for c in range(NT):
                dve.wait_ge(scores_relu, c + 1)
                dve.tensor_reduce(adm[:, 0, c:c + 1], adp[:, c, :], AX.X, ALU.max, negate=True).then_inc(scores_max, 1)

            def softmax_sums():
                for c in range(NT):
                    dve.wait_ge(scores_exp, c + 1)
                    step.add(dve.tensor_reduce(adm[:, 1, c:c + 1], adp[:, c, :], AX.X, ALU.add))
                step.wait()
                dep(dve.reciprocal(adm[:, 2, :], adm[:, 1, :]))
                for c in range(NT):
                    step.add(dve.tensor_scalar(adp[:, c, :], adp[:, c, :], adm[:, 2, c:c + 1], None, ALU.mult))
                step.wait()
                for c in range(NT):
                    step.add(dve.tensor_reduce(adm[:, 3, c:c + 1], adp[:, c, :], AX.X, ALU.add))
                step.wait()
                for c in range(NT):
                    step.add(dve.tensor_scalar(dia[:, c, :], ident[:, :], adm[:, 3, c:c + 1], None, ALU.mult))
                step.wait()
                dve.sem_inc(scores_dia, 1)
                dve.wait_ge(adj_sums_p, 1)
                dep(dve.tensor_copy(s1_bc[:, :], bank[6][:, :]))
                step.add(dve.tensor_tensor(s2_bc[:, :], s1_bc[:, :], s1_bc[:, :], ALU.mult))

            def after(n):
                if n == -1:
                    step.add(dve.tensor_tensor(gW_sb[:, 1, :], gW_sb[:, 1, :], gW_sb[:, 3, :], ALU.add))
                    step.add(dve.tensor_tensor(gW_sb[:, 2, :], gW_sb[:, 2, :], gW_sb[:, 4, :], ALU.add))
                    dve.wait_ge(soft_sums_p, 1)
                    dep(dve.tensor_copy(a1_bc[:, :], bank[7][:, :]))
                    dep(dve.tensor_tensor(a2_bc[:, :], a1_bc[:, :], a1_bc[:, :], ALU.mult))
                    dve.sem_inc(factors, 1)

            def norm_stats(q):
                for t in range(QB * NT):
                    step.add(dve.bn_stats(stA[:, t, :], xs[:, bass.ds(q * (QB * GW) + t * D, D)]))
                step.wait()
                for t in range(QB * NT):
                    ins = dve.bn_aggr(mvA[:, t, :], stA[:, t, :])
                    if t < QB * NT - 1:
                        step.add(ins)
                ins.then_inc(aln_stats, 1)

            def norm_apply(q):
                dve.wait_ge(aln_rstd, q + 1)
                half = (q % 2) * (QB * GW)
                for t in range(QB * NT):
                    ins = dve.tensor_scalar(big[:, bass.ds(half + t * D, D)],
                                            xs[:, bass.ds(q * (QB * GW) + t * D, D)],
                                            mvA[:, t, 0:1], rsA[:, t:t + 1], ALU.subtract, ALU.mult)
                    if t < QB * NT - 1:
                        step.add(ins)
                ins.then_inc(aln_f, 1)

            def residual(q):
                half = (q % 2) * (QB * GW)
                for c in range(NT):
                    z = bank[4 + c % 2]
                    dve.wait_ge(a_z, q * NT + c + 1)
                    ta = ft[c % 2][:, :, :]
                    tb = ft[2 + c % 2][:, :, :]
                    step.add(dve.tensor_tensor(ta, z[:, :].rearrange("p (b d) -> p b d", b=QB), b2_bc[:, :, :], ALU.add))
                    step.wait()
                    dve.sem_inc(a_zfree, 1)
                    f = big[:, bass.ds(half, QB * GW)].rearrange("p (b c d) -> p b c d", b=QB, c=NT)[:, :, c, :]
                    dep(dve.scalar_tensor_tensor(out=tb, in0=ta, scalar=0.0, in1=f, op0=ALU.max, op1=ALU.add))
                    xv = xs[:, bass.ds(q * (QB * GW), QB * GW)].rearrange("p (b c d) -> p b c d", b=QB, c=NT)[:, :, c, :]
                    dep(dve.scalar_tensor_tensor(out=xv, in0=tb, scalar=0.5, in1=xv, op0=ALU.mult, op1=ALU.add))

            dve.wait_ge(x_in[0], 16)
            norm_stats(0)
            norm_apply(0)
            softmax_sums()
            dve.wait_ge(w_first, W_FIRST)
            for q in range(1, 4):
                dve.wait_ge(x_in[q], 16)
            AQ = B // QB
            step.clear()
            with dve.Fori(0, AQ - 1) as q:
                norm_stats(q + 1)
                norm_apply(q + 1)
                residual(q)
                step.clear()
            residual(AQ - 1)
            dve.wait_ge(w_in, W_IN)
            dve.wait_ge(offset_p, 1)
            dep(dve.tensor_tensor(b1_of, b1_of, bank[5][:, 0:ED * HC].rearrange("p (e c) -> p e c", e=ED), ALU.add))

            def stats(k, g, src=None):
                for c in range(NT):
                    step.add(dve.bn_stats(st[k][:, c, :], src[:, c, :] if src is not None
                                          else xs[:, bass.ds(g * GW + c * D, D)]))
                step.wait()
                for c in range(NT):
                    ins = dve.bn_aggr(mv[k][:, c, :], st[k][:, c, :])
                    if c < NT - 1:
                        step.add(ins)
                ins.then_inc(ln_stats[k], 1)

            def apply(k, n, g, src=None, dst=None):
                dve.wait_ge(ln_rstd[k], n)
                for c in range(NT):
                    ins = dve.tensor_scalar(ft[k][:, c, :] if dst is None else big[:, bass.ds(g * GW + c * D, D)],
                                            src[:, c, :] if src is not None else xs[:, bass.ds(g * GW + c * D, D)],
                                            mv[k][:, c, 0:1], rs[k][:, c:c + 1], ALU.subtract, ALU.mult)
                    if c < NT - 1:
                        step.add(ins)
                ins.then_inc(ln_f[k], 1)

            def top2(k, E, bias, dst):
                dep(dve.tensor_tensor(lg[k][:, :, 0:E], bank[2][:, 0:NT * E].rearrange("p (c e) -> p c e", c=NT),
                                      bias[:, :, :], ALU.add))
                for c in range(NT):
                    step.add(dve.max(mx[k][:, c, :], lg[k][:, c, :]))
                step.wait()
                for c in range(NT):
                    step.add(dve.max_index(ix[k][:, c, :], mx[k][:, c, :], lg[k][:, c, :]))
                step.wait()
                dep(dve.tensor_copy(ixf[k][:, :, :], ix[k][:, :, 0:2].rearrange("p c j -> p j c")))
                for j in range(2):
                    step.add(dve.tensor_tensor(dst[j], iota8[:, :, :],
                                               ixf[k][:, j, :].unsqueeze(2).broadcast_to([P, NT, 8]), ALU.is_equal))
                step.wait()

            def mix(k, dst, a, b):
                for j, w in ((0, a), (1, b)):
                    step.add(dve.tensor_tensor(oh[k][:, j, :, :], oh[k][:, j, :, :],
                                               w.unsqueeze(2).broadcast_to([P, NT, 8]), ALU.mult))
                step.wait()
                return dve.tensor_tensor(dst, oh[k][:, 0, :, :], oh[k][:, 1, :, :], ALU.add)

            def route_b1(n):
                dve.wait_ge(b_lp, n + 1)
                top2(0, EB, rb2_bc, [oh[0][:, j, :, :] for j in range(2)])
                step.add(dve.tensor_tensor(dl[0][:, :, :], lg[0][:, :, :],
                                           mx[0][:, :, 0:1].broadcast_to([P, NT, 8]), ALU.subtract))
                step.wait()
                dve.sem_inc(b_ask, 1)

            def route_b2(n):
                w = wt[0]
                dve.wait_ge(b_exp, n * 2 + 1)
                dep(dve.tensor_reduce(w[:, 0, :], ex[0][:, :, :], AX.X, ALU.add))
                dep(dve.reciprocal(w[:, 1, :], w[:, 0, :]))
                dep(dve.tensor_tensor(dl[0][:, :, :], ex[0][:, :, :], oh[0][:, 1, :, :], ALU.mult))
                dep(dve.tensor_reduce(w[:, 2, :], dl[0][:, :, :], AX.X, ALU.add))
                dep(dve.tensor_tensor(w[:, 2, :], w[:, 2, :], w[:, 1, :], ALU.mult))
                step.add(dve.tensor_tensor(w[:, 3, :], w[:, 2, :], w[:, 1, :], ALU.subtract))
                step.wait()
                dve.sem_inc(b_ask, 1)

            def route_b3(n):
                w = wt[0]
                dve.wait_ge(b_exp, n * 2 + 2)
                dep(dve.tensor_scalar(w[:, 5, :], w[:, 4, :], 1.0, None, ALU.add))
                dep(dve.reciprocal(w[:, 6, :], w[:, 5, :]))
                dep(dve.tensor_tensor(w[:, 7, :], w[:, 4, :], w[:, 6, :], ALU.mult))

            def route_b4(n):
                w = wt[0]
                if not (isinstance(n, int) and n == 0):
                    dve.wait_ge(b_cp, n)
                dep(mix(0, cB[:, :, :], w[:, 6, :], w[:, 7, :]))
                dve.sem_inc(b_c, 1)

            def combine(n, e):
                dve.wait_ge(b_op, n * EB + (e + 1))
                for c in range(NT):
                    xc = xs[:, bass.ds(n * GW + c * D, D)]
                    step.add(dve.scalar_tensor_tensor(out=xc, in0=bank[5 + e % 2][:, c * D:(c + 1) * D],
                                                      scalar=cB[:, c, e:e + 1], in1=xc, op0=ALU.mult, op1=ALU.add))
                step.wait()
                dve.sem_inc(b_ofree, 1)

            def body(n, cur, prev, nxt, part):
                m = n - 1
                if prev:
                    stats(1, m)
                    apply(1, n, m)
                if nxt:
                    stats(0, n + 1)
                if cur:
                    combine(n, 0)
                    dve.wait_ge(b_bias, n + 1)
                    xg = grp(xs, n)
                    dep(dve.tensor_tensor(xg, xg, bank[1][:, :], ALU.add))
                    dve.sem_inc(b_biasfree, 1)
                if nxt:
                    apply(0, n + 2, n + 1)
                if cur:
                    combine(n, 1)
                    combine(n, 2)
                if prev:
                    dve.wait_ge(c_p, n)
                    dve.wait_ge(c_b, n)
                    xg = grp(xs, m)
                    dep(dve.tensor_tensor(xg, xg, bank[7][:, :], ALU.add))
                    stats(2, m)
                if nxt:
                    route_b1(n + 1)
                if prev:
                    apply(2, n, m)
                if nxt:
                    route_b2(n + 1)
                if cur:
                    combine(n, 3)
                if prev:
                    dve.wait_ge(ln_f[2], n)
                    stats(3, m, ft[2])
                if nxt:
                    route_b3(n + 1)
                if cur:
                    combine(n, 4)
                if prev:
                    apply(3, n, m, ft[2], big)
                    dve.wait_ge(d_lp, n)
                    top2(1, ED, br_bc, [ohD[:, j, :, bass.ds(m * NT, NT)].rearrange("p e c -> p c e") for j in range(2)])
                    w = wt[1]
                    dep(dve.tensor_tensor(w[:, 0, :], mx[1][:, :, 1], mx[1][:, :, 0], ALU.subtract))
                    dve.sem_inc(d_ask, 1)
                if cur:
                    combine(n, 5)
                if nxt:
                    route_b4(n + 1)
                if prev:
                    dve.wait_ge(d_exp, n)
                    dep(dve.tensor_scalar(w[:, 2, :], w[:, 1, :], 1.0, None, ALU.add))
                    dep(dve.reciprocal(w[:, 3, :], w[:, 2, :]))
                    dep(dve.tensor_tensor(w[:, 4, :], w[:, 1, :], w[:, 3, :], ALU.mult))
                    dep(dve.tensor_copy(wD[:, :, bass.ds(m * NT, NT)], w[:, 3:5, :]))

            def at_route(part):
                g0, g1 = PARTS[part]
                MTp = NT * (g1 - g0)
                w = ED * MTp
                b0 = sum(NBS[:part])
                nb = NBS[part]

                def et(t):
                    return t[:, 0:w].rearrange("p (e t) -> p e t", e=ED)

                ohs = [ohD[:, j, :, g0 * NT:g1 * NT] for j in range(2)]
                dep(dve.tensor_tensor(et(seen), ohs[0], ohs[1], ALU.add))
                dve.sem_inc(seen_ready, 1)
                dve.wait_ge(ranks_p, part + 1)
                dep(dve.tensor_copy(tot[:, 0:w], bank[7][:, w:2 * w]))
                dep(dve.tensor_tensor_scan(cum[:, 0:w], onesr[:, 0:w], tot[:, 0:w], 0.0, ALU.mult, ALU.add))
                step.add(dve.tensor_tensor(cum[:, 0:w], cum[:, 0:w], tot[:, 0:w], ALU.subtract))
                dep(dve.tensor_reduce(cnt[:, 0, :], et(tot), AX.X, ALU.add))
                dep(dve.tensor_scalar(cnti[:, 0, :], cnt[:, 0, :], float(BLK - 1), None, ALU.add))
                dep(dve.tensor_scalar(cnti[:, 1, :], cnti[:, 0, :], BLK.bit_length() - 1, None, ALU.arith_shift_right))
                dep(dve.tensor_copy(cnt[:, 1, :], cnti[:, 1, :]))
                dep(dve.tensor_tensor_scan(cnt[:, 2, :], onesr[:, 0:ED], cnt[:, 1, :], 0.0, ALU.mult, ALU.add))
                dep(dve.tensor_tensor(cnt[:, 3, :], cnt[:, 2, :], cnt[:, 1, :], ALU.subtract))
                dep(dve.tensor_scalar(cnt[:, 4, :], cnt[:, 3, :], float(BLK), None, ALU.mult))
                dep(dve.tensor_tensor(cnt[:, 5, :], cnt[:, 4, :], et(cum)[:, :, 0], ALU.subtract))
                dep(dve.tensor_tensor(et(cum), et(cum), cnt[:, 5, :].unsqueeze(2).broadcast_to([P, ED, MTp]), ALU.add))
                dep(dve.tensor_tensor(cum[:, 0:w], cum[:, 0:w], bank[7][:, 0:w], ALU.add))
                for j in range(2):
                    dep(dve.tensor_tensor(et(tot), ohs[j], et(cum), ALU.mult))
                    dep(dve.tensor_reduce(seen[:, j * MTp:(j + 1) * MTp], et(tot).rearrange("p e t -> p t e"), AX.X, ALU.add))
                dep(dve.tensor_copy(slot[:, :, g0 * NT:g1 * NT], seen[:, 0:2 * MTp].rearrange("p (j t) -> p j t", j=2)))
                dep(dve.tensor_tensor(blkc[:, 0:nb, :], cnt[0:1, 2, 0:ED - 1].unsqueeze(1).broadcast_to([1, nb, ED - 1]),
                                      iotab[:, 0:nb].unsqueeze(2).broadcast_to([1, nb, ED - 1]), ALU.is_le))
                dep(dve.tensor_reduce(blkf[:, b0:b0 + nb], blkc[:, 0:nb, :], AX.X, ALU.add))
                dep(dve.tensor_copy(blk_e[:, b0:b0 + nb], blkf[:, b0:b0 + nb]))
                dve.sem_inc(routed, 1)

            pipeline(dve, body, step, at_route, after)

            def expert(j):
                return dve.value_load(blk_e[0:1, bass.ds(j, 1)], min_val=0, max_val=ED - 1)

            def weights1(j, par, e):
                if not (isinstance(j, int) and j < 2):
                    dve.wait_ge(e_h, j * HC - HC)
                dve.tensor_copy(W1s[:, par, :], W1b[:, bass.ds(e, 1), :].rearrange("p a n -> p (a n)")).then_inc(e_w1, 1)

            def weights2(j, par, e):
                if not (isinstance(j, int) and j < 2):
                    dve.wait_ge(e_yp, j - 1)
                    dve.wait_ge(e_y, j - 1)
                dve.tensor_copy(W2s[:, par, :], W2b[:, bass.ds(e, 1), :].rearrange("p a n -> p (a n)")).then_inc(e_w2, 1)

            def inputs(j, par):
                dve.wait_ge(e_tp, j + 1)
                dve.tensor_copy(xT[:, par, :], bank[0][:, 0:BLK]).then_inc(e_xT, 1)

            def results(j, par):
                dve.wait_ge(e_yp, j + 1)
                if not (isinstance(j, int) and j < 2):
                    dve.wait_ge(y_out[par], (j // 2) * 16)
                dve.tensor_tensor(yb[:, par, :, :], bank[5 + par][:, 0:BT * D].rearrange("p (t d) -> p t d", t=BT),
                                  W2s[:, par, H:H + D].unsqueeze(1).broadcast_to([P, BT, D]), ALU.add).then_inc(e_y, 1)

            def block(j, par):
                inputs(j + 1, 1 - par)
                e = expert(j + 1)
                weights1(j + 1, 1 - par, e)
                results(j - 1, 1 - par)
                weights2(j + 1, 1 - par, e)

            def combine_last(m, k, turn):
                dve.wait_ge(gathered[k], turn * (16 * 2 * NT) + 16 * 2 * NT)
                dep(dve.tensor_copy(wc[:, :, :], wD[:, :, bass.ds(m * NT, NT)]))
                for j in range(2):
                    for c in range(NT):
                        xc = xs[:, bass.ds(m * GW + c * D, D)]
                        step.add(dve.scalar_tensor_tensor(out=xc, in0=yg[k][:, j, c, :], scalar=wc[:, j, c:c + 1],
                                                          in1=xc, op0=ALU.mult, op1=ALU.add))
                    step.wait()
                dve.sem_inc(g_used, 1)
                dve.sem_inc(x_done, 1)

            dve.wait_ge(gains, ED)
            dve.wait_ge(staged, SPLIT)
            inputs(0, 0)
            for j in range(2):
                e = expert(j)
                weights1(j, j, e)
                weights2(j, j, e)
            inputs(1, 1)
            pairs = NB_ALL // 2
            before = (NBS[0] + 1) // 2 + 1
            block(1, 1)
            with dve.Fori(1, before) as i:
                for par in range(2):
                    block(i * 2 + par, par)
            step.clear()
            with dve.Fori(0, SPLIT // 2) as i:
                for k in range(2):
                    for q in range(GAP):
                        for par in range(2):
                            block(i * (4 * GAP) + (2 * (before + k * GAP + q) + par), par)
                    combine_last(i * 2 + k, k, i)
                step.clear()
            after = before + SPLIT * GAP
            with dve.Fori(after, pairs - 1) as i:
                for par in range(2):
                    block(i * 2 + par, par)
            block(NB_ALL - 2, 0)
            results(NB_ALL - 2, 0)
            results(NB_ALL - 1, 1)
            step.clear()
            with dve.Fori(SPLIT // 2, G // 2) as i:
                for k in range(2):
                    combine_last(i * 2 + k, k, i)
                step.clear()


_OUT = ((16, 512, 128), "float32")


def kernel(**inputs):
    import numpy as np
    import concourse.bacc as bacc
    from concourse import mybir as mb
    from concourse.bass_utils import run_bass_kernel_spmd as run

    a = {k: np.asarray(v) for k, v in inputs.items()}
    e_last = a["L1_ffn_W1"].shape[0]
    nodes = a["adj"].shape[0]
    tiles = nodes // 128

    def rows(v, n):
        return np.broadcast_to(v[None, None, :], (128, n, v.shape[0]))

    laid = {
        "x": a["x"], "adjT": a["adj"].T,
        "w1_loop": a["L0_gnn_w1_loop"], "w1_neigh": a["L0_gnn_w1_neigh"], "b1": a["L0_gnn_b1"][:, None],
        "w2_loop": a["L0_gnn_w2_loop"], "w2_neigh": a["L0_gnn_w2_neigh"], "b2": rows(a["L0_gnn_b2"], 4),
        "rw1": a["L0_ffn_router_w1"], "rb1": a["L0_ffn_router_b1"][:, None],
        "rw2": a["L0_ffn_router_w2"], "rb2": rows(a["L0_ffn_router_b2"], tiles),
        "ew1": a["L0_ffn_expert_w1"], "eb1": a["L0_ffn_expert_b1"].T,
        "ew2": a["L0_ffn_expert_w2"], "eb2": a["L0_ffn_expert_b2"].T,
        "ew3": a["L0_ffn_expert_w3"], "eb3": a["L0_ffn_expert_b3"],
        "nv1T": a["L1_gnn_node_vec1"].T, "nv2": a["L1_gnn_node_vec2"],
        "gW": a["L1_gnn_W"], "gb": rows(a["L1_gnn_b"], tiles),
        "Wr": a["L1_ffn_Wr"], "br": rows(a["L1_ffn_br"], tiles),
        "lngT": a["L1_ffn_ln_g"].T, "lnbT": a["L1_ffn_ln_b"].T,
        "W1": a["L1_ffn_W1"], "b1T": a["L1_ffn_b1"].reshape(e_last, -1, 128).transpose(2, 0, 1),
        "W2": a["L1_ffn_W2"].reshape(e_last, -1, 128, 128).transpose(2, 0, 1, 3).reshape(128, e_last, -1), "b2e": np.broadcast_to(a["L1_ffn_b2"][None], (128, e_last, 128)),
    }
    nc = bacc.Bacc("TRN2", target_bir_lowering=False, num_devices=1)
    arrays, args = {}, []
    for name, v in laid.items():
        v = np.ascontiguousarray(v)
        arrays[f"in_{name}"] = v
        args.append(nc.dram_tensor(f"in_{name}", v.shape, mb.dt.from_np(v.dtype), kind="ExternalInput").ap())
    args.append(nc.dram_tensor("out_0", _OUT[0], mb.dt.from_np(np.dtype(_OUT[1])), kind="ExternalOutput").ap())
    program(nc, *args)
    r = run(nc, [arrays], core_ids=[0])
    return r.results[0]["out_0"]
```

```python
from contextlib import ExitStack

import concourse.bass as bass
from concourse import mybir

P = 128
F32 = mybir.dt.float32
U32 = mybir.dt.uint32
I32 = mybir.dt.int32
ALU = mybir.AluOpType
ACT = mybir.ActivationFunctionType
AX = mybir.AxisListType
LN_EPS = 1e-5
PAD_LOGIT = -1e30
SPLIT = 8
GAP = 2


class Steps:

    def __init__(self, eng, sem):
        self.eng, self.sem, self.n = eng, sem, 0

    def add(self, ins):
        ins.then_inc(self.sem, 1)
        self.n += 1

    def wait(self):
        self.eng.wait_ge(self.sem, self.n)

    def clear(self):
        if self.n:
            self.wait()
        self.eng.sem_clear(self.sem)
        self.n = 0


def program(nc, x, adjT, w1_loop, w1_neigh, b1, w2_loop, w2_neigh, b2, rw1, rb1, rw2, rb2, ew1, eb1, ew2, eb2,
            ew3, eb3, nv1T, nv2, gW, gb, Wr, br, lngT, lnbT, W1, b1T, W2, b2e, out):
    B, N, D = x.shape
    T = B * N
    NT = N // P
    G = T // N
    GW = NT * D
    EB = ew1.shape[0]
    RH = rw1.shape[1]
    ED = W1.shape[0]
    H = W1.shape[2]
    HC = H // P
    RANK = nv1T.shape[0]
    QB = 4
    PARTS = ((0, SPLIT), (SPLIT, G))
    BLK = 256
    BT = BLK // P
    NBS = [((g1 - g0) * N * 2 + ED * (BLK - 1)) // BLK for g0, g1 in PARTS]
    NB_ALL = sum(NBS)
    MT = max(g1 - g0 for g0, g1 in PARTS) * NT
    assert NB_ALL % 2 == 0
    FILLS = sum(-(-(nb * BLK) // T) for nb in NBS)
    Xd = [nc.dram_tensor(f"x_slots{k}", [nb * BLK, D], F32, kind="Internal").ap() for k, nb in enumerate(NBS)]
    Yd = [nc.dram_tensor(f"y_slots{k}", [nb * BLK, D], F32, kind="Internal").ap() for k, nb in enumerate(NBS)]

    ctx = ExitStack()
    with ctx:
        def sb(name, shape, dt=F32):
            return ctx.enter_context(nc.sbuf_tensor(name, shape, dt))

        def ps(name, shape):
            return ctx.enter_context(nc.psum_tensor(name, shape, F32))

        def carve(t, *shapes):
            at, pieces = 0, []
            for shape in shapes:
                size = 1
                for k in shape:
                    size *= k
                piece = t[:, at:at + size]
                if len(shape) == 2:
                    piece = piece.rearrange("p (a b) -> p a b", a=shape[0])
                elif len(shape) == 3:
                    piece = piece.rearrange("p (a b c) -> p a b c", a=shape[0], b=shape[1])
                pieces.append(piece)
                at += size
            return pieces

        def sem(name):
            return ctx.enter_context(nc.semaphore(name))

        xs = sb("xs", [P, G * GW])
        big = sb("big", [P, G * GW])
        fA = big[:, 0:2 * QB * GW].rearrange("p (h b n) -> p h b n", h=2, b=QB)
        adp = big[:, 8 * GW:8 * GW + NT * N].rearrange("p (c n) -> p c n", c=NT)
        dia = big[:, 12 * GW:12 * GW + NT * P].rearrange("p (c n) -> p c n", c=NT)
        adjT_sb = sb("adjT_sb", [P, NT, N])
        wA = sb("wA", [P, 4, D])
        b1_sb = sb("b1_sb", [P, 1])
        b2_bc = sb("b2_bc", [P, QB, D])
        rw1_sb = sb("rw1_sb", [P, RH])
        rb1_sb = sb("rb1_sb", [RH, 1])
        rw2_sb = sb("rw2_sb", [RH, EB])
        rb2_bc = sb("rb2_bc", [P, NT, EB])
        ew1_sb = sb("ew1_sb", [P, EB, D])
        ew2_sb = sb("ew2_sb", [P, EB, D])
        ew3_sb = sb("ew3_sb", [P, EB, D])
        eb1_sb = sb("eb1_sb", [P, EB])
        eb2_sb = sb("eb2_sb", [P, EB])
        eb3_sb = sb("eb3_sb", [EB, D])
        nv1T_sb = big[0:RANK, 14 * GW:14 * GW + N]
        nv2_sb = big[0:RANK, 15 * GW:15 * GW + N]
        gW_sb = sb("gW_sb", [P, 7, D])
        gb_bc = sb("gb_bc", [P, NT, D])
        Wr_sb = sb("Wr_sb", [P, ED])
        br_bc = sb("br_bc", [P, NT, ED])
        lngT_sb = sb("lngT_sb", [P, ED])
        lnbT_sb = sb("lnbT_sb", [P, ED])
        W1b = sb("W1b", [P, ED, H + HC])
        W2b = sb("W2b", [P, ED, H + D])
        W1_sb = W1b[:, :, 0:H]
        b1_of = W1b[:, :, H:H + HC]
        ident = sb("ident", [P, P])
        ones = sb("ones", [P, P])
        iota8 = sb("iota8", [P, NT, 8])
        eps = sb("eps", [P, QB * NT])
        neg_half = sb("neg_half", [P, QB * NT])
        s1_bc = sb("s1_bc", [P, N])
        s2_bc = sb("s2_bc", [P, N])
        a1_bc = sb("a1_bc", [P, N])
        a2_bc = sb("a2_bc", [P, N])
        adm = sb("adm", [P, 4, NT])
        st = [sb(f"st{k}", [P, NT, 6]) for k in range(4)]
        mv = [sb(f"mv{k}", [P, NT, 2]) for k in range(4)]
        ve = [sb(f"ve{k}", [P, NT]) for k in range(4)]
        rs = [sb(f"rs{k}", [P, NT]) for k in range(4)]
        ft = [sb(f"ft{k}", [P, NT, D]) for k in range(4)]
        fT = [sb(f"fT{k}", [P, 2 * N if k == 0 else N]) for k in range(3)]
        stA = sb("stA", [P, QB * NT, 6])
        mvA = sb("mvA", [P, QB * NT, 2])
        veA = sb("veA", [P, QB * NT])
        rsA = sb("rsA", [P, QB * NT])
        work = sb("work", [P, 4 * N])
        uT, fTA = carve(work, (2, N), (2, N))
        xst, seen, tot, cum = carve(work, (2, NT, D), (ED * MT,), (ED * MT,), (ED * MT,))
        hT = sb("hT", [P, 2, HC, N])
        h1A = hT[:, 0]
        gA = hT[:, 1].rearrange("p m (b d) -> p m b d", b=QB)
        rhT = sb("rhT", [RH, N])
        fs_last = [fT[0][:, 0:N], fT[0][:, N:2 * N], ft[0][:, :, :].rearrange("p c d -> p (c d)"),
                   ft[1][:, :, :].rearrange("p c d -> p (c d)")]
        h1T, h2T, fs = carve(hT[:, :, :, :].rearrange("p a b n -> p (a b n)"), (2, N), (2, N), (4, N))
        lg = [sb(f"lg{k}", [P, NT, 8]) for k in range(2)]
        mx = [sb(f"mx{k}", [P, NT, 8]) for k in range(2)]
        ix = [sb(f"ix{k}", [P, NT, 8], U32) for k in range(2)]
        ixf = [sb(f"ixf{k}", [P, 2, NT]) for k in range(2)]
        oh = sb("oh", [P, 2, NT, 8])
        dl = sb("dl", [P, NT, 8])
        ex = sb("ex", [P, NT, 8])
        wt = sb("wt", [P, 8, NT])
        cB = sb("cB", [P, NT, 8])
        ohD = sb("ohD", [P, 2, ED, G * NT])
        wD = sb("wD", [P, 2, G * NT])
        gapD = sb("gapD", [P, G * NT])
        slot = sb("slot", [P, 2, G * NT], U32)
        tri = sb("tri", [P, P])
        onesr = sb("onesr", [P, ED * MT])
        cnt = sb("cnt", [P, 6, ED])
        cnti = sb("cnti", [P, 2, ED], I32)
        iotab = sb("iotab", [1, NB_ALL])
        blkc = sb("blkc", [1, NB_ALL, ED - 1])
        blkf = sb("blkf", [1, NB_ALL])
        blk_e = sb("blk_e", [1, NB_ALL], I32)
        wc = sb("wc", [P, 2, NT])
        ist = sb("ist", [P, 2, 2, NT], U32)
        igt = sb("igt", [P, 2, 2, NT], U32)
        W1s, W2s, xb, xT, yb = carve(big[:, 0:SPLIT * GW], (2, H + HC), (2, H + D), (2, BT, D), (2, BLK), (2, BT, D))
        yg = carve(big[:, SPLIT * GW:], (2, NT, D), (2, NT, D))
        cT = sb("cT", [8, N])

        bank = [ps(f"bank{k}", [P, 512]) for k in range(8)]

        x_in = [sem(f"x_in{q}") for q in range(4)]
        nv_in, w_first, w_in = sem("nv_in"), sem("w_first"), sem("w_in")
        x_out = sem("x_out")
        pool_step = sem("pool_step")
        dve_step = sem("dve_step")
        consts = sem("consts")
        scores_p, scores_relu, scores_max, scores_exp, scores_dia = [
            sem("scores_" + s) for s in "p relu max exp dia".split()]
        adj_sums_p, soft_sums_p, offset_p, factors, gains = [
            sem(s) for s in "adj_sums_p soft_sums_p offset_p factors gains".split()]
        ln_stats = [sem(f"ln_stats{k}") for k in range(4)]
        ln_rstd = [sem(f"ln_rstd{k}") for k in range(4)]
        ln_f = [sem(f"ln_f{k}") for k in range(4)]
        turned = [sem(f"turned{k}") for k in range(4)]
        turned_sb = [sem(f"turned_sb{k}") for k in range(4)]
        aln_stats, aln_rstd, aln_f = sem("aln_stats"), sem("aln_rstd"), sem("aln_f")
        a_fp, a_fT, a_up, a_uT, a_hp, a_h, a_gp, a_g, a_z, a_zfree = [
            sem("a_" + s) for s in "fp fT up uT hp h gp g z zfree".split()]
        b_rp, b_rh, b_lp, b_hp, b_h, b_op, b_ofree, b_c, b_cp, b_cT, b_bias, b_biasfree, b_ask, b_exp = [
            sem("b_" + s) for s in "rp rh lp hp h op ofree c cp cT bias biasfree ask exp".split()]
        c_fs, c_p, c_b = [sem("c_" + s) for s in "fs p b".split()]
        d_lp, d_exp = [sem("d_" + s) for s in "lp exp".split()]
        x_done = sem("x_done")
        slots_set = sem("slots_set")
        seen_ready, ranks_p, routed = sem("seen_ready"), sem("ranks_p"), sem("routed")
        staged, scattered = sem("staged"), [sem(f"scattered{k}") for k in range(2)]
        xb_in = [sem(f"xb_in{k}") for k in range(2)]
        y_out = [sem(f"y_out{k}") for k in range(2)]
        gathered = [sem(f"gathered{k}") for k in range(2)]
        g_used = sem("g_used")
        e_tp, e_xT, e_w1, e_w2, e_hp, e_h, e_yp, e_y = [
            sem("e_" + s) for s in "tp xT w1 w2 hp h yp y".split()]

        xr = x.rearrange("b (c p) d -> p b c d", p=P)
        xs_v = xs[:, :].rearrange("p (b c d) -> p b c d", b=B, c=NT)

        first_loads = [
            (adjT_sb[:, :, :], adjT.rearrange("(c p) n -> p c n", p=P)),
            (wA[:, 0, :], w1_loop), (wA[:, 1, :], w1_neigh), (wA[:, 2, :], w2_loop), (wA[:, 3, :], w2_neigh),
            (b1_sb[:, :], b1), (b2_bc[:, :, :], b2),
        ]
        loads = [
            (rw1_sb[:, :], rw1), (rb1_sb[:, :], rb1), (rw2_sb[:, :], rw2),
            (rb2_bc[:, :, :], rb2),
            (ew1_sb[:, :, :], ew1.rearrange("e d h -> d e h")),
            (ew2_sb[:, :, :], ew2.rearrange("e d h -> d e h")),
            (ew3_sb[:, :, :], ew3.rearrange("e d h -> d e h")),
            (eb1_sb[:, :], eb1), (eb2_sb[:, :], eb2), (eb3_sb[:, :], eb3),
            (gW_sb[:, :, :], gW.rearrange("(k p) n -> p k n", p=P)),
            (gb_bc[:, :, :], gb),
            (Wr_sb[:, :], Wr), (br_bc[:, :, :], br),
            (lngT_sb[:, :], lngT), (lnbT_sb[:, :], lnbT),
            (W1_sb, W1.rearrange("e d h -> d e h")),
            (b1_of, b1T),
            (W2b[:, :, 0:H], W2),
            (W2b[:, :, H:H + D], b2e),
        ]
        W_FIRST = 16 * len(first_loads)
        W_IN = 16 * len(loads)

        HID = [(1, 0), (1, 1), (2, 0), (1, 2), (2, 1), (1, 3), (2, 2), (1, 4), (2, 3), (1, 5), (2, 4), (2, 5)]
        NH = len(HID)

        assert G == 2 * SPLIT and SPLIT % 2 == 0
        PER_SCATTER = 16 * 2 * NT
        BEFORE = (SPLIT - 1, 1)
        SCATTERED = [[PER_SCATTER * b for b in BEFORE], [PER_SCATTER * (b + SPLIT // 2) for b in BEFORE]]

        BESIDE = 10
        assert NBS[0] > BESIDE

        block = ctx.enter_context(nc.Block())

        def fT0(m):
            return fT[0][:, bass.ds((m % 2) * N, N)]

        def grp(t, g, w=GW):
            return t[:, bass.ds(g * w, w)]

        def pipeline(eng, body, steps=None, at_route=None, after=None):
            def loop(a, b, part):
                if a < b:
                    if steps:
                        steps.clear()
                    with eng.Fori(a, b) as n:
                        body(n, True, True, 2, part)
                        if steps:
                            steps.clear()

            body(-1, False, False, 2, 0)
            if after:
                after(-1)
            body(0, True, False, 2, 0)
            if after:
                after(0)
            loop(1, SPLIT + 1, 0)
            if at_route:
                at_route()
            body(SPLIT + 1, True, True, 2, 1)
            loop(SPLIT + 2, G - 2, 1)
            body(G - 2, True, True, 1, 1)
            body(G - 1, True, True, 0, 1)

        @block.sync
        def _(sp):
            sp.dma_start(nv1T_sb, nv1T).then_inc(nv_in, 16)
            sp.dma_start(nv2_sb, nv2).then_inc(nv_in, 16)

            def load_x(q):
                sp.dma_start(xs_v[:, QB * q:QB * q + QB], xr[:, QB * q:QB * q + QB]).then_inc(x_in[q], 16)

            load_x(0)
            for dst, src in first_loads:
                sp.dma_start(dst, src).then_inc(w_first, 16)
            for q in range(1, 4):
                load_x(q)
            for dst, src in loads:
                sp.dma_start(dst, src).then_inc(w_in, 16)
            x_rows = x.rearrange("b n d -> (b n) d").rearrange("(p r) d -> p (r d)", p=P)
            for part, nb in enumerate(NBS):
                rows = nb * BLK // P
                Xi = Xd[part].rearrange("(p r) d -> p (r d)", p=P)
                for r in range(0, rows, G * NT):
                    k = min(G * NT, rows - r)
                    sp.dma_start(Xi[:, r * D:(r + k) * D], x_rows[:, 0:k * D]).then_inc(slots_set, 16)

            def rows_of(slots, j, part):
                return slots[part][bass.ds((j - sum(NBS[:part])) * BLK, BLK), :].rearrange("(t p) d -> p t d", p=P)

            def load(j, par, part):
                if not (isinstance(j, int) and j < 2):
                    sp.wait_ge(e_tp, j - 1)
                sp.dma_start(xb[:, par, :, :], rows_of(Xd, j, part)).then_inc(xb_in[par], 16)

            def store(j, par, part):
                sp.wait_ge(e_y, j + 1)
                sp.dma_start(rows_of(Yd, j, part), yb[:, par, :, :]).then_inc(y_out[par], 16)

            def part_in(part):
                for k in range(2):
                    if SCATTERED[part][k]:
                        sp.wait_ge(scattered[k], SCATTERED[part][k])

            AHEAD = 4
            cut = NBS[0]
            part_in(0)
            for j in range(AHEAD + 1):
                load(j, j % 2, 0)

            def step(t):
                if t + AHEAD == cut:
                    part_in(1)
                if t + AHEAD < NB_ALL:
                    load(t + AHEAD, (t + AHEAD) % 2, int(t + AHEAD >= cut))
                store(t - 1, (t - 1) % 2, int(t - 1 >= cut))

            def steps(t0, t1, part):
                with sp.Fori(0, (t1 - t0) // 2) as i:
                    for k in range(2):
                        load(i * 2 + (t0 + k + AHEAD), (1 + k + AHEAD) % 2, part)
                        store(i * 2 + (t0 + k - 1), k, part)
                return t0 + (t1 - t0) // 2 * 2

            for t in range(steps(1, cut - AHEAD, 0), cut + 1):
                step(t)
            t = cut + 1
            if t % 2 == 0:
                step(t)
                t += 1
            for t in range(steps(t, NB_ALL - AHEAD, 1), NB_ALL + 1):
                step(t)
            with sp.Fori(0, G) as g:
                sp.wait_ge(x_done, g + 1)
                sp.dma_start(out[bass.ds(g, 1)].rearrange("b (c p) d -> p (b c) d", p=P),
                             grp(xs, g).rearrange("p (c d) -> p c d", c=NT)).then_inc(x_out, 16)
            sp.wait_ge(x_out, 16 * G)

        @block.gpsimd
        def _(pool):
            step = Steps(pool, pool_step)
            step.add(pool.memset(ident[:, :], 0.0))
            pool.memset(ones[:, :], 1.0).then_inc(consts, 1)
            pool.memset(neg_half[:, :], -0.5).then_inc(consts, 1)
            pool.memset(eps[:, :], LN_EPS).then_inc(consts, 1)
            for k in range(2):
                pool.memset(lg[k][:, :, :], PAD_LOGIT).then_inc(consts, 1)
            pool.memset(onesr[:, :], 1.0).then_inc(consts, 1)
            step.add(pool.memset(tri[:, :], 0.0))
            pool.iota(iotab[:, :], [[1, NB_ALL]], channel_multiplier=0,
                      allow_small_or_imprecise_dtypes=True).then_inc(consts, 1)
            pool.iota(iota8[:, :, :], [[0, NT], [1, 8]], channel_multiplier=0,
                      allow_small_or_imprecise_dtypes=True).then_inc(consts, 1)
            step.wait()
            pool.affine_select(out=ident[:, :], in_=ident[:, :], compare_op=ALU.not_equal, fill=1.0, base=0,
                               pattern=[[-1, P]], channel_multiplier=1).then_inc(consts, 1)
            pool.affine_select(out=tri[:, :], in_=tri[:, :], compare_op=ALU.is_ge, fill=1.0, base=0,
                               pattern=[[-1, P]], channel_multiplier=1).then_inc(consts, 1)
            pool.wait_ge(consts, 10)

            step.clear()
            with pool.Fori(0, B // QB) as q:
                pool.wait_ge(aln_stats, q + 1)
                step.add(pool.tensor_tensor(veA[:, :], mvA[:, :, 1], eps[:, :], ALU.add))
                step.wait()
                pool.tensor_tensor(rsA[:, :], veA[:, :], neg_half[:, :], ALU.pow).then_inc(aln_rstd, 1)
                step.clear()

            def rstd(k, n):
                pool.wait_ge(ln_stats[k], n)
                step.add(pool.tensor_tensor(ve[k][:, :], mv[k][:, :, 1], eps[:, 0:NT], ALU.add))
                step.wait()
                pool.tensor_tensor(rs[k][:, :], ve[k][:, :], neg_half[:, 0:NT], ALU.pow).then_inc(ln_rstd[k], 1)

            def stage(m, k, turn):
                if not (isinstance(turn, int) and turn == 0):
                    pool.wait_ge(scattered[k], turn * PER_SCATTER)
                pool.tensor_copy(xst[:, k, :, :].rearrange("p c d -> p (c d)"), grp(big, m)).then_inc(staged, 1)
                pool.wait_ge(staged, m + 1)
                step.add(pool.tensor_copy(ist[:, k, :, :], slot[:, :, bass.ds(m * NT, NT)]))
                step.wait()

            SENDS = (1, 2, 3)

            def send(k, part, tiles):
                for c in tiles:
                    for j in range(2):
                        pool.indirect_dma_start(Xd[part][:, :],
                                                bass.IndirectOffsetOnAxis(ap=ist[:, k, j, c:c + 1], axis=0),
                                                xst[:, k, c, :], None).then_inc(scattered[k], 16)

            def scaled(n, dst):
                pool.wait_ge(turned_sb[1], n)
                for k, by in enumerate((s1_bc, s2_bc, a1_bc, a2_bc)):
                    pool.tensor_tensor(dst[k], fT[1][:, :], by[:, :], ALU.mult).then_inc(c_fs, 1)
                pool.wait_ge(ln_f[1], n)
                pool.tensor_tensor(grp(xs, n - 1), grp(xs, n - 1), gb_bc[:, :, :].rearrange("p a b -> p (a b)"),
                                   ALU.add).then_inc(c_b, 1)

            def body(n, cur, prev, nxt, part):
                if prev:
                    scaled(n, [fs[:, k, :] for k in range(4)])
                if part == 1:
                    if isinstance(n, int) and n == SPLIT + 1:
                        pool.wait_ge(slots_set, 16 * FILLS)
                        pool.wait_ge(routed, 1)
                    m = n - (SPLIT + 1)
                    stage(m, 0, m)
                    send(0, 0, range(0, SENDS[0]))
                if nxt == 2:
                    rstd(0, n + 3)
                if prev:
                    rstd(2, n)
                if part == 1 and nxt:
                    send(0, 0, range(SENDS[0], SENDS[1]))
                if nxt == 0:
                    stage(SPLIT - 1, 1, 0)
                    send(0, 0, range(SENDS[0], 3 * NT // 4))
                if prev:
                    rstd(3, n)
                if part == 1:
                    send(0, 0, range(SENDS[1], SENDS[2]) if nxt else range(3 * NT // 4, NT))
                if cur:
                    rstd(1, n + 1)
                if part == 1 and nxt:
                    send(0, 0, range(SENDS[2], NT))

            def after(n):
                if n == 0:
                    pool.wait_ge(factors, 1)

            rstd(0, 1)
            pool.wait_ge(w_in, W_IN)
            pipeline(pool, body, step, None, after)
            send(1, 0, range(NT))
            scaled(G, fs_last)
            rstd(2, G)
            rstd(3, G)
            pool.wait_ge(routed, 2)
            for k in range(2):
                stage(SPLIT + k, k, BEFORE[k])
                send(k, 1, range(NT))
            step.clear()
            with pool.Fori(1, (G - SPLIT) // 2) as i:
                for k in range(2):
                    stage(i * 2 + (SPLIT + k), k, i + BEFORE[k])
                    send(k, 1, range(NT))
                step.clear()

            def gather(m, k, turn, part):
                if not (isinstance(turn, int) and turn == 0):
                    pool.wait_ge(g_used, m - 1)
                step.add(pool.tensor_copy(igt[:, k, :, :], slot[:, :, bass.ds(m * NT, NT)]))
                step.wait()
                for c in range(NT):
                    for j in range(2):
                        pool.indirect_dma_start(yg[k][:, j, c, :], None, Yd[part][:, :],
                                                bass.IndirectOffsetOnAxis(ap=igt[:, k, j, c:c + 1], axis=0)
                                                ).then_inc(gathered[k], 16)

            for part, (g0, g1) in enumerate(PARTS):
                done = sum(NBS[:part + 1])
                pool.wait_ge(y_out[0], 16 * ((done + 1) // 2))
                pool.wait_ge(y_out[1], 16 * (done // 2))
                if part == 0:
                    gather(0, 0, 0, part)
                    gather(1, 1, 0, part)
                a = 1 if part == 0 else g0 // 2
                step.clear()
                with pool.Fori(a, g1 // 2) as i:
                    for k in range(2):
                        gather(i * 2 + k, k, 1, part)
                    step.clear()

        @block.tensor
        def _(pe):
            mm = pe.matmul
            pe.wait_ge(consts, 10)
            pe.wait_ge(nv_in, 32)
            for c in range(NT):
                mm(bank[4 + c][:, :], nv1T_sb[:, c * P:(c + 1) * P], nv2_sb,
                   start=True, stop=True).then_inc(scores_p, 1)
            pe.wait_ge(w_first, W_FIRST)
            pe.wait_ge(scores_relu, NT)
            for m in range(NT):
                ins = mm(bank[6][:, :], ones[:, :], adjT_sb[:, m, :], start=(m == 0), stop=(m == NT - 1))
            ins.then_inc(adj_sums_p, 1)

            def first_layer(q, half, i):
                f = fA[:, half]
                done = q * QB

                def turn(b):
                    if b == 0:
                        pe.wait_ge(aln_f, q + 1)
                    if b > 0:
                        pe.wait_ge(a_fT, done + b)
                    for c in range(NT):
                        ins = pe.transpose(bank[0][:, c * P:(c + 1) * P], f[:, b, c * D:(c + 1) * D], ident[:, :])
                    ins.then_inc(a_fp, 1)

                def neigh(b):
                    if b > 0:
                        pe.wait_ge(a_uT, done + b)
                    for m in range(NT):
                        ins = mm(bank[1][:, :], f[:, b, m * D:(m + 1) * D], adjT_sb[:, m, :],
                                 start=(m == 0), stop=(m == NT - 1))
                    ins.then_inc(a_up, 1)

                def hidden(b):
                    pe.wait_ge(a_fT, done + b + 1)
                    pe.wait_ge(a_uT, done + b + 1)
                    if b > 0:
                        pe.wait_ge(a_h, done + b)
                    mm(bank[2][:, :], wA[:, 0, :], fTA[:, b % 2, :], start=True, stop=False)
                    mm(bank[2][:, :], wA[:, 1, :], uT[:, b % 2, :], start=False, stop=True).then_inc(a_hp, 1)

                def second(b):
                    pe.wait_ge(a_h, done + b + 1)
                    if b > 0:
                        pe.wait_ge(a_g, done + b)
                    for m in range(NT):
                        ins = mm(bank[3][:, m * D:(m + 1) * D], h1A[:, b, m * P:(m + 1) * P], wA[:, 3, :],
                                 start=True, stop=True)
                    ins.then_inc(a_gp, 1)

                turn(0)
                neigh(0)
                turn(1)
                hidden(0)
                neigh(1)
                turn(2)
                hidden(1)
                second(0)
                neigh(2)
                turn(3)
                hidden(2)
                second(1)
                neigh(3)
                second(2)
                hidden(3)
                second(3)
                pe.wait_ge(a_g, done + QB)
                for c in range(NT):
                    pe.wait_ge(a_zfree, q * NT + (c + 1))
                    z = bank[4 + c % 2]
                    for m in range(NT):
                        mm(z[:, :], adjT_sb[:, m, c * P:(c + 1) * P], gA[:, m, :, :], start=(m == 0), stop=(m == NT - 1))
                    for b in range(QB):
                        ins = mm(z[:, b * D:(b + 1) * D], h1A[:, b, c * P:(c + 1) * P], wA[:, 2, :],
                                 start=False, stop=True, skip_group_check=True)
                    ins.then_inc(a_z, 1)

            with pe.Fori(0, B // QB // 2) as i:
                for half in range(2):
                    first_layer(i * 2 + half, half, i)

            def turn(k, n, bank_free=None, z=bank[0]):
                if bank_free:
                    pe.wait_ge(*bank_free)
                pe.wait_ge(ln_f[k], n)
                for c in range(NT):
                    ins = pe.transpose(z[:, c * P:(c + 1) * P], ft[k][:, c, :], ident[:, :])
                ins.then_inc(turned[k], 1)

            def graph(n, f):
                pe.wait_ge(c_fs, n * 4)
                for c in range(NT):
                    for k in range(5):
                        ins = mm(bank[7][:, c * D:(c + 1) * D], (fT[1] if k == 0 else f[k - 1])[:, c * P:(c + 1) * P],
                                 gW_sb[:, k if k < 3 else k + 2, :], start=(k == 0), stop=(k == 4))
                ins.then_inc(c_p, 1)

            def logits(n, z):
                pe.wait_ge(turned_sb[2], n)
                for c in range(NT):
                    ins = mm(z[:, c * ED:(c + 1) * ED], fT[2][:, c * P:(c + 1) * P], Wr_sb[:, :],
                             start=True, stop=True)
                ins.then_inc(d_lp, 1)

            def hid(n, j):
                layer, e = HID[j]
                if layer == 2:
                    pe.wait_ge(b_h, n * NH + (HID.index((1, e)) + 1))
                if not (isinstance(n, int) and n == 0 and j < 2):
                    pe.wait_ge(b_h, n * NH + (j - 1))
                w, f = (ew1_sb, fT0(n)) if layer == 1 else (ew2_sb, h1T[:, e % 2, :])
                mm(bank[3 + j % 2][:, :], w[:, e, :], f, start=True, stop=True).then_inc(b_hp, 1)

            def outp(n, e):
                pe.wait_ge(b_h, n * NH + (HID.index((2, e)) + 1))
                if not (isinstance(n, int) and n == 0 and e < 2):
                    pe.wait_ge(b_ofree, n * EB + (e - 1))
                for c in range(NT):
                    ins = mm(bank[5 + e % 2][:, c * D:(c + 1) * D], h2T[:, e % 2, c * P:(c + 1) * P], ew3_sb[:, e, :],
                             start=True, stop=True)
                ins.then_inc(b_op, 1)

            def offsets():
                for e in range(ED):
                    for c in range(HC):
                        k = e * HC + c
                        ins = mm(bank[0][:, k:k + 1], W1b[:, e, c * P:(c + 1) * P], lnbT_sb[:, e:e + 1],
                                 start=True, stop=True)
                ins.then_inc(offset_p, 1)

            def ranks(part):
                g0, g1 = PARTS[part]
                w = ED * NT * (g1 - g0)
                pe.wait_ge(seen_ready, part + 1)
                mm(bank[7][:, 0:w], tri[:, :], seen[:, 0:w], start=True, stop=True)
                mm(bank[7][:, w:2 * w], ones[:, :], seen[:, 0:w], start=True, stop=True,
                   skip_group_check=True).then_inc(ranks_p, 1)

            def body(n, cur, prev, nxt, part):
                if cur:
                    hid(n, 0)
                    hid(n, 1)
                    hid(n, 2)
                    hid(n, 3)
                    hid(n, 4)
                    hid(n, 5)
                    if isinstance(n, int) and n == SPLIT + 1:
                        offsets()
                        ranks(0)
                    pe.wait_ge(b_c, n + 1)
                    for c in range(NT):
                        ins = pe.transpose(bank[1][0:8, c * P:(c + 1) * P], cB[:, c, :], ident[:, :])
                    ins.then_inc(b_cp, 1)
                    outp(n, 0)
                if prev:
                    turn(1, n)
                if cur:
                    hid(n, 6)
                    pe.wait_ge(b_cT, n + 1)
                    for c in range(NT):
                        ins = mm(bank[1][:, c * D:(c + 1) * D], cT[0:EB, c * P:(c + 1) * P], eb3_sb[:, :],
                                 start=True, stop=True)
                    ins.then_inc(b_bias, 1)
                    outp(n, 1)
                if nxt:
                    turn(0, n + 2, (turned_sb[1], n) if prev else None)
                if cur:
                    hid(n, 7)
                    hid(n, 8)
                    outp(n, 2)
                if nxt:
                    pe.wait_ge(turned_sb[0], n + 2)
                    if cur:
                        pe.wait_ge(b_biasfree, n + 1)
                    mm(bank[1][0:RH, :], rw1_sb[:, :], fT0(n + 1), start=True, stop=True).then_inc(b_rp, 1)
                if prev:
                    if part == 1:
                        pe.wait_ge(routed, 1)
                    graph(n, [fs[:, k, :] for k in range(4)])
                if nxt:
                    pe.wait_ge(b_rh, n + 2)
                    for c in range(NT):
                        ins = mm(bank[2][:, c * EB:(c + 1) * EB], rhT[:, c * P:(c + 1) * P], rw2_sb[:, :],
                                 start=True, stop=True)
                    ins.then_inc(b_lp, 1)
                if cur:
                    hid(n, 9)
                    hid(n, 10)
                    outp(n, 3)
                    hid(n, 11)
                if prev:
                    turn(2, n, (turned_sb[0], n + 2) if nxt else (turned_sb[1], n))
                if cur:
                    outp(n, 4)
                if prev:
                    logits(n, bank[2])
                if cur:
                    outp(n, 5)

            pe.wait_ge(scores_dia, 1)
            for c in range(NT):
                ins = mm(bank[7][:, c * P:(c + 1) * P], ones[:, :], dia[:, c, :], start=True, stop=True)
            ins.then_inc(soft_sums_p, 1)
            pe.wait_ge(w_in, W_IN)

            def after(n):
                if n == -1:
                    pe.wait_ge(a_zfree, G + 2)

            pipeline(pe, body, None, None, after)
            turn(1, G, None, bank[7])

            def turn_block(j, par):
                pe.wait_ge(xb_in[par], (j // 2) * 16 + 16)
                if not (isinstance(j, int) and j < 1):
                    pe.wait_ge(e_xT, j)
                for t in range(BT):
                    ins = pe.transpose(bank[0][:, t * P:(t + 1) * P], xb[:, par, t, :], ident[:, :])
                ins.then_inc(e_tp, 1)

            def hidden(j, par):
                pe.wait_ge(e_xT, j + 1)
                pe.wait_ge(e_w1, j + 1)
                if not (isinstance(j, int) and j < 2):
                    pe.wait_ge(e_h, j * HC - HC)
                for c in range(HC):
                    z = bank[1 + 2 * par + c // 2]
                    ins = mm(z[:, (c % 2) * BLK:(c % 2 + 1) * BLK], W1s[:, par, c * P:(c + 1) * P], xT[:, par, :],
                             start=True, stop=True)
                    if c % 2:
                        ins.then_inc(e_hp, 1)

            def outer(j, par):
                pe.wait_ge(e_h, j * HC + HC)
                pe.wait_ge(e_w2, j + 1)
                if not (isinstance(j, int) and j < 2):
                    pe.wait_ge(e_y, j - 1)
                for t in range(BT):
                    for k in range(HC):
                        ins = mm(bank[5 + par][:, t * D:(t + 1) * D], hT[:, par, k, t * P:(t + 1) * P],
                                 W2s[:, par, k * D:(k + 1) * D], start=(k == 0), stop=(k == HC - 1))
                ins.then_inc(e_yp, 1)

            turn_block(0, 0)
            turn_block(1, 1)
            hidden(0, 0)
            turn_block(2, 0)
            hidden(1, 1)
            turn_block(3, 1)
            outer(0, 0)
            beside = {3: lambda: graph(G, fs_last), 5: lambda: turn(2, G, None, bank[7]),
                      6: lambda: logits(G, bank[7]), 7: lambda: ranks(1)}
            for j in range(2, BESIDE):
                hidden(j, j % 2)
                turn_block(j + 2, j % 2)
                outer(j - 1, 1 - j % 2)
                if j in beside:
                    beside[j]()
            with pe.Fori(BESIDE // 2, NB_ALL // 2 - 1) as i:
                for par in range(2):
                    hidden(i * 2 + par, par)
                    turn_block(i * 2 + (par + 2), par)
                    outer(i * 2 + (par - 1), 1 - par)
            j = NB_ALL - 2
            hidden(j, 0)
            outer(j - 1, 1)
            hidden(j + 1, 1)
            outer(j, 0)
            outer(j + 1, 1)

        @block.scalar
        def _(act):
            for c in range(NT):
                act.wait_ge(scores_p, c + 1)
                act.activation(adp[:, c, :], bank[4 + c][:, :], ACT.Relu).then_inc(scores_relu, 1)
            for c in range(NT):
                act.wait_ge(scores_max, c + 1)
                act.activation(adp[:, c, :], adp[:, c, :], ACT.Exp, bias=adm[:, 0, c:c + 1]).then_inc(scores_exp, 1)
            act.wait_ge(w_first, W_FIRST)

            def first_layer(q):
                done = q * QB

                def copies(b):
                    act.wait_ge(a_fp, done + b + 1)
                    if b >= 2:
                        act.wait_ge(a_hp, done + b - 1)
                    act.copy(fTA[:, b % 2, :], bank[0][:, :]).then_inc(a_fT, 1)

                def copies2(b):
                    act.wait_ge(a_up, done + b + 1)
                    act.copy(uT[:, b % 2, :], bank[1][:, :]).then_inc(a_uT, 1)

                def relu(b):
                    act.wait_ge(a_hp, done + b + 1)
                    act.activation(h1A[:, b, :], bank[2][:, :], ACT.Relu, bias=b1_sb[:, :]).then_inc(a_h, 1)

                def second(b):
                    act.wait_ge(a_gp, done + b + 1)
                    act.copy(gA[:, :, b, :], bank[3][:, :].rearrange("p (m d) -> p m d", m=NT)).then_inc(a_g, 1)

                copies(0)
                copies2(0)
                copies(1)
                relu(0)
                copies2(1)
                copies(2)
                relu(1)
                second(0)
                copies2(2)
                copies(3)
                relu(2)
                second(1)
                copies2(3)
                second(2)
                relu(3)
                second(3)

            with act.Fori(0, B // QB) as q:
                first_layer(q)

            def turned_copy(k, n, dst):
                act.wait_ge(turned[k], n)
                act.copy(dst, bank[0][:, :]).then_inc(turned_sb[k], 1)

            def hid(n, j):
                layer, e = HID[j]
                act.wait_ge(b_hp, n * NH + (j + 1))
                if e >= 2 and layer == 1:
                    act.wait_ge(b_hp, n * NH + (HID.index((2, e - 2)) + 1))
                if e >= 2 and layer == 2:
                    act.wait_ge(b_op, n * EB + (e - 1))
                dst, b = (h1T, eb1_sb) if layer == 1 else (h2T, eb2_sb)
                act.activation(dst[:, e % 2, :], bank[3 + j % 2][:, :], ACT.Relu, bias=b[:, e:e + 1]).then_inc(b_h, 1)
                if isinstance(n, int) and n == SPLIT + 1 and j >= NH - ED:
                    e = j - (NH - ED)
                    act.wait_ge(offset_p, 1)
                    act.activation(W1b[:, e, 0:H], W1b[:, e, 0:H], ACT.Copy,
                                   scale=lngT_sb[:, e:e + 1]).then_inc(gains, 1)

            def body(n, cur, prev, nxt, part):
                if cur:
                    hid(n, 0)
                    hid(n, 1)
                    hid(n, 2)
                    hid(n, 3)
                    hid(n, 4)
                    hid(n, 5)
                    act.wait_ge(b_cp, n + 1)
                    act.copy(cT[:, :], bank[1][0:8, :]).then_inc(b_cT, 1)
                if prev:
                    turned_copy(1, n, fT[1][:, :])
                if cur:
                    hid(n, 6)
                if nxt:
                    turned_copy(0, n + 2, fT0(n + 1))
                if cur:
                    hid(n, 7)
                    hid(n, 8)
                if nxt:
                    act.wait_ge(b_rp, n + 2)
                    act.activation(rhT[:, :], bank[1][0:RH, :], ACT.Relu, bias=rb1_sb[:, :]).then_inc(b_rh, 1)
                if cur:
                    hid(n, 9)
                if nxt:
                    act.wait_ge(b_ask, n * 2 + 3)
                    act.activation(ex[:, :, :], dl[:, :, :], ACT.Exp).then_inc(b_exp, 1)
                if cur:
                    hid(n, 10)
                    hid(n, 11)
                if nxt:
                    act.wait_ge(b_ask, n * 2 + 4)
                    act.activation(wt[:, 4, :], wt[:, 3, :], ACT.Exp).then_inc(b_exp, 1)
                if prev:
                    turned_copy(2, n, fT[2][:, :])

            act.wait_ge(w_in, W_IN)
            pipeline(act, body)
            def gelus(j, par):
                for c in range(HC):
                    if c % 2 == 0:
                        act.wait_ge(e_hp, j * 2 + (c // 2 + 1))
                    if c == 0 and not (isinstance(j, int) and j < 2):
                        act.wait_ge(e_yp, j - 1)
                    act.activation(hT[:, par, c, 0:BLK], bank[1 + 2 * par + c // 2][:, (c % 2) * BLK:(c % 2 + 1) * BLK],
                                   ACT.Gelu, bias=W1s[:, par, H + c:H + c + 1]).then_inc(e_h, 1)

            for j in range(BESIDE):
                gelus(j, j % 2)
            act.wait_ge(seen_ready, 2)
            act.activation(wD[:, 1, :], gapD[:, :], ACT.Exp).then_inc(d_exp, 1)
            with act.Fori(BESIDE // 2, NB_ALL // 2) as i:
                for par in range(2):
                    gelus(i * 2 + par, par)

        @block.vector
        def _(dve):
            step = Steps(dve, dve_step)

            def dep(ins):
                step.add(ins)
                step.wait()

            dve.sem_inc(a_zfree, 2)
            dve.wait_ge(consts, 10)
            for c in range(NT):
                dve.wait_ge(scores_relu, c + 1)
                dve.tensor_reduce(adm[:, 0, c:c + 1], adp[:, c, :], AX.X, ALU.max, negate=True).then_inc(scores_max, 1)

            def softmax_sums():
                for c in range(NT):
                    dve.wait_ge(scores_exp, c + 1)
                    step.add(dve.tensor_reduce(adm[:, 1, c:c + 1], adp[:, c, :], AX.X, ALU.add))
                step.wait()
                dep(dve.reciprocal(adm[:, 2, :], adm[:, 1, :]))
                for c in range(NT):
                    step.add(dve.tensor_scalar(adp[:, c, :], adp[:, c, :], adm[:, 2, c:c + 1], None, ALU.mult))
                step.wait()
                for c in range(NT):
                    step.add(dve.tensor_reduce(adm[:, 3, c:c + 1], adp[:, c, :], AX.X, ALU.add))
                step.wait()
                for c in range(NT):
                    step.add(dve.tensor_scalar(dia[:, c, :], ident[:, :], adm[:, 3, c:c + 1], None, ALU.mult))
                step.wait()
                dve.sem_inc(scores_dia, 1)
                dve.wait_ge(adj_sums_p, 1)
                dep(dve.tensor_copy(s1_bc[:, :], bank[6][:, :]))
                step.add(dve.tensor_tensor(s2_bc[:, :], s1_bc[:, :], s1_bc[:, :], ALU.mult))

            def after(n):
                if n == -1:
                    step.add(dve.tensor_tensor(gW_sb[:, 1, :], gW_sb[:, 1, :], gW_sb[:, 3, :], ALU.add))
                    step.add(dve.tensor_tensor(gW_sb[:, 2, :], gW_sb[:, 2, :], gW_sb[:, 4, :], ALU.add))
                    dve.wait_ge(soft_sums_p, 1)
                    dep(dve.tensor_copy(a1_bc[:, :], bank[7][:, :]))
                    dep(dve.tensor_tensor(a2_bc[:, :], a1_bc[:, :], a1_bc[:, :], ALU.mult))
                    dve.sem_inc(factors, 1)

            def norm_stats(q):
                for t in range(QB * NT):
                    step.add(dve.bn_stats(stA[:, t, :], xs[:, bass.ds(q * (QB * GW) + t * D, D)]))
                step.wait()
                for t in range(QB * NT):
                    ins = dve.bn_aggr(mvA[:, t, :], stA[:, t, :])
                    if t < QB * NT - 1:
                        step.add(ins)
                ins.then_inc(aln_stats, 1)

            def norm_apply(q):
                dve.wait_ge(aln_rstd, q + 1)
                half = (q % 2) * (QB * GW)
                for t in range(QB * NT):
                    ins = dve.tensor_scalar(big[:, bass.ds(half + t * D, D)],
                                            xs[:, bass.ds(q * (QB * GW) + t * D, D)],
                                            mvA[:, t, 0:1], rsA[:, t:t + 1], ALU.subtract, ALU.mult)
                    if t < QB * NT - 1:
                        step.add(ins)
                ins.then_inc(aln_f, 1)

            def residual(q):
                half = (q % 2) * (QB * GW)
                for c in range(NT):
                    z = bank[4 + c % 2]
                    dve.wait_ge(a_z, q * NT + c + 1)
                    ta = ft[1][:, :, :]
                    tb = ft[2 + c % 2][:, :, :]
                    step.add(dve.tensor_tensor(ta, z[:, :].rearrange("p (b d) -> p b d", b=QB), b2_bc[:, :, :], ALU.add))
                    step.wait()
                    dve.sem_inc(a_zfree, 1)
                    f = big[:, bass.ds(half, QB * GW)].rearrange("p (b c d) -> p b c d", b=QB, c=NT)[:, :, c, :]
                    dep(dve.scalar_tensor_tensor(out=tb, in0=ta, scalar=0.0, in1=f, op0=ALU.max, op1=ALU.add))
                    xv = xs[:, bass.ds(q * (QB * GW), QB * GW)].rearrange("p (b c d) -> p b c d", b=QB, c=NT)[:, :, c, :]
                    dep(dve.scalar_tensor_tensor(out=xv, in0=tb, scalar=0.5, in1=xv, op0=ALU.mult, op1=ALU.add))

            dve.wait_ge(x_in[0], 16)
            norm_stats(0)
            norm_apply(0)
            softmax_sums()
            dve.wait_ge(w_first, W_FIRST)
            for q in range(1, 4):
                dve.wait_ge(x_in[q], 16)
            AQ = B // QB
            step.clear()
            with dve.Fori(0, AQ - 1) as q:
                norm_stats(q + 1)
                norm_apply(q + 1)
                residual(q)
                step.clear()
            def stats(k, g, src=None):
                for c in range(NT):
                    step.add(dve.bn_stats(st[k][:, c, :], src[:, c, :] if src is not None
                                          else xs[:, bass.ds(g * GW + c * D, D)]))
                step.wait()
                for c in range(NT):
                    ins = dve.bn_aggr(mv[k][:, c, :], st[k][:, c, :])
                    if c < NT - 1:
                        step.add(ins)
                ins.then_inc(ln_stats[k], 1)

            def apply(k, n, g, src=None, dst=None):
                dve.wait_ge(ln_rstd[k], n)
                for c in range(NT):
                    ins = dve.tensor_scalar(ft[k][:, c, :] if dst is None else big[:, bass.ds(g * GW + c * D, D)],
                                            src[:, c, :] if src is not None else xs[:, bass.ds(g * GW + c * D, D)],
                                            mv[k][:, c, 0:1], rs[k][:, c:c + 1], ALU.subtract, ALU.mult)
                    if c < NT - 1:
                        step.add(ins)
                ins.then_inc(ln_f[k], 1)

            def top2(k, E, bias, dst, z=bank[2]):
                dep(dve.tensor_tensor(lg[k][:, :, 0:E], z[:, 0:NT * E].rearrange("p (c e) -> p c e", c=NT),
                                      bias[:, :, :], ALU.add))
                for c in range(NT):
                    step.add(dve.max(mx[k][:, c, :], lg[k][:, c, :]))
                step.wait()
                for c in range(NT):
                    step.add(dve.max_index(ix[k][:, c, :], mx[k][:, c, :], lg[k][:, c, :]))
                step.wait()
                dep(dve.tensor_copy(ixf[k][:, :, :], ix[k][:, :, 0:2].rearrange("p c j -> p j c")))
                for j in range(2):
                    step.add(dve.tensor_tensor(dst[j], iota8[:, :, :],
                                               ixf[k][:, j, :].unsqueeze(2).broadcast_to([P, NT, 8]), ALU.is_equal))
                step.wait()

            def mix(dst, a, b):
                for j, w in ((0, a), (1, b)):
                    step.add(dve.tensor_tensor(oh[:, j, :, :], oh[:, j, :, :],
                                               w.unsqueeze(2).broadcast_to([P, NT, 8]), ALU.mult))
                step.wait()
                return dve.tensor_tensor(dst, oh[:, 0, :, :], oh[:, 1, :, :], ALU.add)

            def route_b1(n):
                dve.wait_ge(b_lp, n + 1)
                top2(0, EB, rb2_bc, [oh[:, j, :, :] for j in range(2)])
                step.add(dve.tensor_tensor(dl[:, :, :], lg[0][:, :, :],
                                           mx[0][:, :, 0:1].broadcast_to([P, NT, 8]), ALU.subtract))
                step.wait()
                dve.sem_inc(b_ask, 1)

            def route_b2(n):
                w = wt
                dve.wait_ge(b_exp, n * 2 + 1)
                dep(dve.tensor_reduce(w[:, 0, :], ex[:, :, :], AX.X, ALU.add))
                dep(dve.reciprocal(w[:, 1, :], w[:, 0, :]))
                dep(dve.tensor_tensor(dl[:, :, :], ex[:, :, :], oh[:, 1, :, :], ALU.mult))
                dep(dve.tensor_reduce(w[:, 2, :], dl[:, :, :], AX.X, ALU.add))
                dep(dve.tensor_tensor(w[:, 2, :], w[:, 2, :], w[:, 1, :], ALU.mult))
                step.add(dve.tensor_tensor(w[:, 3, :], w[:, 2, :], w[:, 1, :], ALU.subtract))
                step.wait()
                dve.sem_inc(b_ask, 1)

            def route_b3(n):
                w = wt
                dve.wait_ge(b_exp, n * 2 + 2)
                dep(dve.tensor_scalar(w[:, 5, :], w[:, 4, :], 1.0, None, ALU.add))
                dep(dve.reciprocal(w[:, 6, :], w[:, 5, :]))
                dep(dve.tensor_tensor(w[:, 7, :], w[:, 4, :], w[:, 6, :], ALU.mult))

            def route_b4(n):
                w = wt
                if not (isinstance(n, int) and n == 0):
                    dve.wait_ge(b_cp, n)
                dep(mix(cB[:, :, :], w[:, 6, :], w[:, 7, :]))
                dve.sem_inc(b_c, 1)

            def combine(n, e):
                dve.wait_ge(b_op, n * EB + (e + 1))
                for c in range(NT):
                    xc = xs[:, bass.ds(n * GW + c * D, D)]
                    step.add(dve.scalar_tensor_tensor(out=xc, in0=bank[5 + e % 2][:, c * D:(c + 1) * D],
                                                      scalar=cB[:, c, e:e + 1], in1=xc, op0=ALU.mult, op1=ALU.add))
                step.wait()
                dve.sem_inc(b_ofree, 1)

            def graph(n, m):
                dve.wait_ge(c_p, n)
                dve.wait_ge(c_b, n)
                xg = grp(xs, m)
                dep(dve.tensor_tensor(xg, xg, bank[7][:, :], ALU.add))
                stats(2, m)

            def choose(n, m, z):
                dve.wait_ge(d_lp, n)
                top2(1, ED, br_bc, [ohD[:, j, :, bass.ds(m * NT, NT)].rearrange("p e c -> p c e") for j in range(2)], z)
                dep(dve.tensor_tensor(gapD[:, bass.ds(m * NT, NT)], mx[1][:, :, 1], mx[1][:, :, 0], ALU.subtract))

            def body(n, cur, prev, nxt, part):
                m = n - 1
                if cur:
                    combine(n, 0)
                    dve.wait_ge(b_bias, n + 1)
                    xg = grp(xs, n)
                    dep(dve.tensor_tensor(xg, xg, bank[1][:, :], ALU.add))
                    dve.sem_inc(b_biasfree, 1)
                    combine(n, 1)
                    combine(n, 2)
                if nxt == 2:
                    stats(0, n + 2)
                if prev:
                    graph(n, m)
                if nxt:
                    route_b1(n + 1)
                if prev:
                    apply(2, n, m)
                if nxt:
                    route_b2(n + 1)
                if cur:
                    combine(n, 3)
                if prev:
                    dve.wait_ge(ln_f[2], n)
                    stats(3, m, ft[2])
                if nxt:
                    route_b3(n + 1)
                if nxt == 2:
                    apply(0, n + 3, n + 2)
                if cur:
                    combine(n, 4)
                    combine(n, 5)
                    stats(1, n)
                if nxt:
                    route_b4(n + 1)
                if cur:
                    apply(1, n + 1, n)
                if prev:
                    choose(n, m, bank[2])
                    apply(3, n, m, ft[2], big)

            def cut(part):
                g0, g1 = PARTS[part]
                MTp = NT * (g1 - g0)
                return g0, g1, MTp, ED * MTp, [ohD[:, j, :, g0 * NT:g1 * NT] for j in range(2)]

            def et(t, w):
                return t[:, 0:w].rearrange("p (e t) -> p e t", e=ED)

            def seen_of(part):
                g0, g1, MTp, w, ohs = cut(part)
                dep(dve.tensor_tensor(et(seen, w), ohs[0], ohs[1], ALU.add))
                dve.sem_inc(seen_ready, 1)

            def counts_of(part):
                g0, g1, MTp, w, ohs = cut(part)
                dve.wait_ge(ranks_p, part + 1)
                dep(dve.tensor_copy(tot[:, 0:w], bank[7][:, w:2 * w]))
                step.add(dve.tensor_tensor_scan(cum[:, 0:w], onesr[:, 0:w], tot[:, 0:w], 0.0, ALU.mult, ALU.add))
                dep(dve.tensor_reduce(cnt[:, 0, :], et(tot, w), AX.X, ALU.add))
                step.add(dve.tensor_tensor(cum[:, 0:w], cum[:, 0:w], tot[:, 0:w], ALU.subtract))
                dep(dve.tensor_scalar(cnti[:, 0, :], cnt[:, 0, :], float(BLK - 1), None, ALU.add))
                dep(dve.tensor_scalar(cnti[:, 1, :], cnti[:, 0, :], BLK.bit_length() - 1, None, ALU.arith_shift_right))
                dep(dve.tensor_copy(cnt[:, 1, :], cnti[:, 1, :]))
                dep(dve.tensor_tensor_scan(cnt[:, 2, :], onesr[:, 0:ED], cnt[:, 1, :], 0.0, ALU.mult, ALU.add))
                dep(dve.tensor_tensor(cnt[:, 3, :], cnt[:, 2, :], cnt[:, 1, :], ALU.subtract))
                dep(dve.tensor_scalar(cnt[:, 4, :], cnt[:, 3, :], float(BLK), None, ALU.mult))
                dep(dve.tensor_tensor(cnt[:, 5, :], cnt[:, 4, :], et(cum, w)[:, :, 0], ALU.subtract))
                dep(dve.tensor_tensor(cum[:, 0:w], cum[:, 0:w], bank[7][:, 0:w], ALU.add))

            def slots_of(part):
                g0, g1, MTp, w, ohs = cut(part)
                dep(dve.tensor_tensor(et(cum, w), et(cum, w), cnt[:, 5, :].unsqueeze(2).broadcast_to([P, ED, MTp]), ALU.add))
                for j in range(2):
                    dep(dve.tensor_tensor(et(tot, w), ohs[j], et(cum, w), ALU.mult))
                    dep(dve.tensor_reduce(seen[:, j * MTp:(j + 1) * MTp], et(tot, w).rearrange("p e t -> p t e"), AX.X, ALU.add))
                dep(dve.tensor_copy(slot[:, :, g0 * NT:g1 * NT], seen[:, 0:2 * MTp].rearrange("p (j t) -> p j t", j=2)))
                dve.sem_inc(routed, 1)

            def blocks_of(part):
                b0, nb = sum(NBS[:part]), NBS[part]
                dep(dve.tensor_tensor(blkc[:, 0:nb, :], cnt[0:1, 2, 0:ED - 1].unsqueeze(1).broadcast_to([1, nb, ED - 1]),
                                      iotab[:, 0:nb].unsqueeze(2).broadcast_to([1, nb, ED - 1]), ALU.is_le))
                dep(dve.tensor_reduce(blkf[:, b0:b0 + nb], blkc[:, 0:nb, :], AX.X, ALU.add))
                dep(dve.tensor_copy(blk_e[:, b0:b0 + nb], blkf[:, b0:b0 + nb]))

            def at_route():
                dve.wait_ge(offset_p, 1)
                dep(dve.tensor_tensor(b1_of, b1_of, bank[0][:, 0:ED * HC].rearrange("p (e c) -> p e c", e=ED), ALU.add))
                seen_of(0)
                counts_of(0)
                slots_of(0)
                blocks_of(0)

            stats(0, 0)
            apply(0, 1, 0)
            residual(AQ - 1)
            dve.wait_ge(w_in, W_IN)
            pipeline(dve, body, step, at_route, after)

            def expert(j):
                return dve.value_load(blk_e[0:1, bass.ds(j, 1)], min_val=0, max_val=ED - 1)

            def weights1(j, par, e):
                if not (isinstance(j, int) and j < 2):
                    dve.wait_ge(e_h, j * HC - HC)
                dve.tensor_copy(W1s[:, par, :], W1b[:, bass.ds(e, 1), :].rearrange("p a n -> p (a n)")).then_inc(e_w1, 1)

            def weights2(j, par, e):
                if not (isinstance(j, int) and j < 2):
                    dve.wait_ge(e_yp, j - 1)
                    dve.wait_ge(e_y, j - 1)
                dve.tensor_copy(W2s[:, par, :], W2b[:, bass.ds(e, 1), :].rearrange("p a n -> p (a n)")).then_inc(e_w2, 1)

            def inputs(j, par):
                dve.wait_ge(e_tp, j + 1)
                dve.tensor_copy(xT[:, par, :], bank[0][:, 0:BLK]).then_inc(e_xT, 1)

            def results(j, par):
                dve.wait_ge(e_yp, j + 1)
                if not (isinstance(j, int) and j < 2):
                    dve.wait_ge(y_out[par], (j // 2) * 16)
                dve.tensor_tensor(yb[:, par, :, :], bank[5 + par][:, 0:BT * D].rearrange("p (t d) -> p t d", t=BT),
                                  W2s[:, par, H:H + D].unsqueeze(1).broadcast_to([P, BT, D]), ALU.add).then_inc(e_y, 1)

            def block(j, par, extra=None, more=True):
                e = expert(j + 1)
                weights1(j + 1, 1 - par, e)
                if more:
                    inputs(j + 2, par)
                if extra:
                    extra()
                results(j - 1, 1 - par)
                weights2(j + 1, 1 - par, e)

            def combine_last(m, k, turn, choices=range(2)):
                if 0 in choices:
                    dve.wait_ge(gathered[k], turn * (16 * 2 * NT) + 16 * 2 * NT)
                    dep(dve.tensor_copy(wc[:, :, :], wD[:, :, bass.ds(m * NT, NT)]))
                for j in choices:
                    for c in range(NT):
                        xc = xs[:, bass.ds(m * GW + c * D, D)]
                        step.add(dve.scalar_tensor_tensor(out=xc, in0=yg[k][:, j, c, :], scalar=wc[:, j, c:c + 1],
                                                          in1=xc, op0=ALU.mult, op1=ALU.add))
                    step.wait()
                if 1 in choices:
                    dve.sem_inc(g_used, 1)
                    dve.sem_inc(x_done, 1)

            dve.wait_ge(turned[1], G)
            dve.tensor_copy(fT[1][:, :], bank[7][:, :]).then_inc(turned_sb[1], 1)
            dve.wait_ge(gains, ED)
            dve.wait_ge(staged, SPLIT)
            inputs(0, 0)
            for j in range(2):
                e = expert(j)
                weights1(j, j, e)
                weights2(j, j, e)
                if j == 0:
                    inputs(1, 1)
            inputs(2, 0)
            pairs = NB_ALL // 2
            before = (NBS[0] + 1) // 2 + 1
            last = G - 1

            def scores_last():
                dve.wait_ge(turned[2], G)
                dve.tensor_copy(fT[2][:, :], bank[7][:, :]).then_inc(turned_sb[2], 1)
                apply(3, G, last, ft[2], big)

            def normalised_last():
                apply(2, G, last)
                dve.wait_ge(ln_f[2], G)
                stats(3, last, ft[2])

            def chosen_last():
                choose(G, last, bank[7])
                seen_of(1)

            beside = {3: lambda: graph(G, last), 4: normalised_last, 5: scores_last, 6: chosen_last,
                      7: lambda: counts_of(1), 8: lambda: slots_of(1), 9: lambda: blocks_of(1)}
            for j in range(1, BESIDE):
                block(j, j % 2, beside.get(j))
            step.clear()
            dve.wait_ge(d_exp, 1)
            dep(dve.tensor_scalar(gapD[:, :], wD[:, 1, :], 1.0, None, ALU.add))
            dep(dve.reciprocal(wD[:, 0, :], gapD[:, :]))
            dep(dve.tensor_tensor(wD[:, 1, :], wD[:, 1, :], wD[:, 0, :], ALU.mult))
            with dve.Fori(BESIDE // 2, before) as i:
                for par in range(2):
                    block(i * 2 + par, par)
            step.clear()
            with dve.Fori(0, SPLIT // 2) as i:
                for k in range(2):
                    for q in range(GAP):
                        for par in range(2):
                            choice = (q * 2 + par) - (2 * GAP - 2)
                            block(i * (4 * GAP) + (2 * (before + k * GAP + q) + par), par,
                                  (lambda: combine_last(i * 2 + k, k, i, [choice])) if choice >= 0 else None)
                step.clear()
            after = before + SPLIT * GAP
            with dve.Fori(after, pairs - 1) as i:
                for par in range(2):
                    block(i * 2 + par, par)
            block(NB_ALL - 2, 0, None, False)
            results(NB_ALL - 2, 0)
            results(NB_ALL - 1, 1)
            step.clear()
            with dve.Fori(SPLIT // 2, G // 2) as i:
                for k in range(2):
                    combine_last(i * 2 + k, k, i)
                step.clear()


_OUT = ((16, 512, 128), "float32")


def kernel(**inputs):
    import numpy as np
    import concourse.bacc as bacc
    from concourse import mybir as mb
    from concourse.bass_utils import run_bass_kernel_spmd as run

    a = {k: np.asarray(v) for k, v in inputs.items()}
    e_last = a["L1_ffn_W1"].shape[0]
    nodes = a["adj"].shape[0]
    tiles = nodes // 128

    def rows(v, n):
        return np.broadcast_to(v[None, None, :], (128, n, v.shape[0]))

    laid = {
        "x": a["x"], "adjT": a["adj"].T,
        "w1_loop": a["L0_gnn_w1_loop"], "w1_neigh": a["L0_gnn_w1_neigh"], "b1": a["L0_gnn_b1"][:, None],
        "w2_loop": a["L0_gnn_w2_loop"], "w2_neigh": a["L0_gnn_w2_neigh"], "b2": rows(a["L0_gnn_b2"], 4),
        "rw1": a["L0_ffn_router_w1"], "rb1": a["L0_ffn_router_b1"][:, None],
        "rw2": a["L0_ffn_router_w2"], "rb2": rows(a["L0_ffn_router_b2"], tiles),
        "ew1": a["L0_ffn_expert_w1"], "eb1": a["L0_ffn_expert_b1"].T,
        "ew2": a["L0_ffn_expert_w2"], "eb2": a["L0_ffn_expert_b2"].T,
        "ew3": a["L0_ffn_expert_w3"], "eb3": a["L0_ffn_expert_b3"],
        "nv1T": a["L1_gnn_node_vec1"].T, "nv2": a["L1_gnn_node_vec2"],
        "gW": a["L1_gnn_W"], "gb": rows(a["L1_gnn_b"], tiles),
        "Wr": a["L1_ffn_Wr"], "br": rows(a["L1_ffn_br"], tiles),
        "lngT": a["L1_ffn_ln_g"].T, "lnbT": a["L1_ffn_ln_b"].T,
        "W1": a["L1_ffn_W1"], "b1T": a["L1_ffn_b1"].reshape(e_last, -1, 128).transpose(2, 0, 1),
        "W2": a["L1_ffn_W2"].reshape(e_last, -1, 128, 128).transpose(2, 0, 1, 3).reshape(128, e_last, -1),
        "b2e": np.broadcast_to(a["L1_ffn_b2"][None], (128, e_last, 128)),
    }
    nc = bacc.Bacc("TRN2", target_bir_lowering=False, num_devices=1)
    arrays, args = {}, []
    for name, v in laid.items():
        v = np.ascontiguousarray(v)
        arrays[f"in_{name}"] = v
        args.append(nc.dram_tensor(f"in_{name}", v.shape, mb.dt.from_np(v.dtype), kind="ExternalInput").ap())
    args.append(nc.dram_tensor("out_0", _OUT[0], mb.dt.from_np(np.dtype(_OUT[1])), kind="ExternalOutput").ap())
    program(nc, *args)
    r = run(nc, [arrays], core_ids=[0])
    return r.results[0]["out_0"]
```
